# Optimizing a Trainium2 kernel written in Bass

```python
import numpy as np
import jax
import jax.numpy as jnp

def _softmax(x, axis=-1):
    return jax.nn.softmax(x, axis=axis)

def _gelu(x):
    return jax.nn.gelu(x, approximate=True)

def _silu(x):
    return jax.nn.silu(x)

def _sigmoid(x):
    return jax.nn.sigmoid(x)

def _layernorm(x, axis=-1, eps=1e-05):
    m = jnp.mean(x, axis=axis, keepdims=True)
    v = jnp.var(x, axis=axis, keepdims=True)
    return (x - m) / jnp.sqrt(v + eps)

def _scatter_add(tgt, idx, src, axis=0):
    return tgt.at[idx].add(src)

def _segment_sum(src, seg, n):
    return jax.ops.segment_sum(src, seg, n)
kernel_name = 'mk_flamingo_gated_d2_seqx_r4_e18758'

def setup_inputs(seed: int=0):
    np.random.seed(seed)
    _w = jnp.asarray

    def _rec_inputs():
        import jax
        import jax.numpy as jnp
        _rk = jax.random.key(seed)
        x = -7.109e-05 + 0.9999 * jax.random.normal(jax.random.fold_in(_rk, 1), (4, 512, 512), jnp.float32)
        _lenS = 512 - jax.random.randint(jax.random.fold_in(_rk, 7), (4,), 0, max(1, 512 // 4) + 1, jnp.int32)
        _lenS2 = 512 - jax.random.randint(jax.random.fold_in(_rk, 8), (4,), 0, max(1, 512 // 4) + 1, jnp.int32)
        _ctx_512P = jax.random.normal(jax.random.fold_in(_rk, 11), (4, 16, 128), jnp.float32)
        _ctx_512c = jax.random.dirichlet(jax.random.fold_in(_rk, 511), 0.3 * jnp.ones((16,), jnp.float32), (4, 512))
        _ctx_512t = jnp.einsum('bsk,bkd->bsd', _ctx_512c, _ctx_512P)
        _ctx_512t = _ctx_512t * jax.lax.rsqrt(jnp.mean(jnp.square(_ctx_512t)) + 1e-12) * 0.953939
        ctx_512 = 2.81802e-05 + 1.00001 * (_ctx_512t + 0.3 * jax.random.normal(jax.random.fold_in(_rk, 611), (4, 512, 128), jnp.float32))
        _g = jax.random.normal(jax.random.fold_in(_rk, 9001), (2, 2), jnp.float32)
        _g = jnp.sign(_g) * jnp.maximum(jnp.abs(_g), 1.0) + (_g == 0) * 1.0
        g_xattn = _g[0]
        g_ffn = _g[1]
        return (x, ctx_512, g_xattn, g_ffn)
    x, ctx_512, g_xattn, g_ffn = _rec_inputs()

    def _L0_xattn_setup():
        import jax, jax.numpy as jnp
        import numpy as np
        EPS = 1e-06
        IMAGE_DIMS = 512
        key = jax.random.key(seed)
        k1, k2, k3 = jax.random.split(key, 3)
        B, I, J, D = (16, 512, 512, 128)
        p = jax.random.normal(k1, (B, I, J), dtype=jnp.float32)
        k_v = jax.random.normal(k2, (B, J, D), dtype=jnp.float32)
        W_k = jax.random.normal(k3, (D, D), dtype=jnp.float32) * (1.0 / np.sqrt(D))
        b_k = jnp.zeros((D,), dtype=jnp.float32)
        ln_gamma = jnp.ones((J,), dtype=jnp.float32)
        ln_beta = jnp.zeros((J,), dtype=jnp.float32)
        return {'p': p, 'k_v': k_v, 'W_k': W_k, 'b_k': b_k, 'ln_gamma': ln_gamma, 'ln_beta': ln_beta}
    _L0_xattn_all = _L0_xattn_setup()
    _L0_xattn_in = {k: v for k, v in _L0_xattn_all.items() if k in ('W_k', 'b_k', 'ln_gamma', 'ln_beta')}
    del _L0_xattn_all

    def _L0_ffn_setup():
        import jax, jax.numpy as jnp
        import numpy as np
        E = 8
        K = 2
        B, L, D = (2, 512, 512)
        I = 192
        IS = 1024
        key = jax.random.key(seed)
        ks = jax.random.split(key, 8)
        s = 0.02
        return {'hidden_states': jax.random.normal(ks[0], (B, L, D), jnp.float32), 'gate_w': jax.random.normal(ks[1], (E, D), jnp.float32) * s, 'gate_up_proj': jax.random.normal(ks[2], (E, 2 * I, D), jnp.float32) * s, 'down_proj': jax.random.normal(ks[3], (E, D, I), jnp.float32) * s, 'shared_gate_w': jax.random.normal(ks[4], (IS, D), jnp.float32) * s, 'shared_up_w': jax.random.normal(ks[5], (IS, D), jnp.float32) * s, 'shared_down_w': jax.random.normal(ks[6], (D, IS), jnp.float32) * s, 'shared_expert_gate_w': jax.random.normal(ks[7], (1, D), jnp.float32) * s}
    _L0_ffn_all = _L0_ffn_setup()
    _L0_ffn_in = {k: v for k, v in _L0_ffn_all.items() if k in ('gate_w', 'gate_up_proj', 'down_proj', 'shared_gate_w', 'shared_up_w', 'shared_down_w', 'shared_expert_gate_w')}
    del _L0_ffn_all

    def _L1_xattn_setup():
        import jax, jax.numpy as jnp
        import numpy as np
        import math
        D_MODEL = 512
        N_HEADS = 16
        N_GROUPS = 4
        HEADS_PER_GROUP = N_HEADS // N_GROUPS
        HEAD_DIM = D_MODEL // N_HEADS
        B, S = (2, 512)
        key = jax.random.key(seed)
        k1, k2, k3, k4, k5 = jax.random.split(key, 5)
        q = jax.random.normal(k1, (B, S, D_MODEL), dtype=jnp.float32)
        k = jax.random.normal(k2, (B, S, N_GROUPS * HEAD_DIM), dtype=jnp.float32)
        v = jax.random.normal(k3, (B, S, N_GROUPS * HEAD_DIM), dtype=jnp.float32)
        lim = 1.0 / math.sqrt(D_MODEL)
        Wc = jax.random.uniform(k4, (D_MODEL, D_MODEL), minval=-lim, maxval=lim, dtype=jnp.float32)
        bc = jax.random.uniform(k5, (D_MODEL,), minval=-lim, maxval=lim, dtype=jnp.float32)
        return {'q': q, 'k': k, 'v': v, 'Wc': Wc, 'bc': bc}
    _L1_xattn_all = _L1_xattn_setup()
    _L1_xattn_in = {k: v for k, v in _L1_xattn_all.items() if k in ('Wc', 'bc')}
    del _L1_xattn_all

    def _L1_ffn_setup():
        import jax, jax.numpy as jnp
        import numpy as np
        E = 16
        D = 512
        H = 352
        HS = 2 * 352
        TOP_K = 6
        ROUTE_SCALE = 1.0
        key = jax.random.key(seed)
        ks = jax.random.split(key, 16)
        s = 0.02
        return {'x': jax.random.normal(ks[0], (4, 256, D), dtype=jnp.float32), 'gate_w': jax.random.normal(ks[1], (E, D), dtype=jnp.float32) * s, 'gate_b': jax.random.normal(ks[2], (E,), dtype=jnp.float32) * s, 'w1': jax.random.normal(ks[3], (E, H, D), dtype=jnp.float32) * s, 'b1': jax.random.normal(ks[4], (E, H), dtype=jnp.float32) * s, 'w2': jax.random.normal(ks[5], (E, D, H), dtype=jnp.float32) * s, 'b2': jax.random.normal(ks[6], (E, D), dtype=jnp.float32) * s, 'w3': jax.random.normal(ks[7], (E, H, D), dtype=jnp.float32) * s, 'b3': jax.random.normal(ks[8], (E, H), dtype=jnp.float32) * s, 'ws1': jax.random.normal(ks[9], (HS, D), dtype=jnp.float32) * s, 'bs1': jax.random.normal(ks[10], (HS,), dtype=jnp.float32) * s, 'ws2': jax.random.normal(ks[11], (D, HS), dtype=jnp.float32) * s, 'bs2': jax.random.normal(ks[12], (D,), dtype=jnp.float32) * s, 'ws3': jax.random.normal(ks[13], (HS, D), dtype=jnp.float32) * s, 'bs3': jax.random.normal(ks[14], (HS,), dtype=jnp.float32) * s}
    _L1_ffn_all = _L1_ffn_setup()
    _L1_ffn_in = {k: v for k, v in _L1_ffn_all.items() if k in ('gate_w', 'gate_b', 'w1', 'b1', 'w2', 'b2', 'w3', 'b3', 'ws1', 'bs1', 'ws2', 'bs2', 'ws3', 'bs3')}
    del _L1_ffn_all
    return {'x': x, 'ctx_512': ctx_512, 'g_xattn': g_xattn, 'g_ffn': g_ffn, 'L0_xattn_W_k': _L0_xattn_in['W_k'], 'L0_xattn_b_k': _L0_xattn_in['b_k'], 'L0_xattn_ln_gamma': _L0_xattn_in['ln_gamma'], 'L0_xattn_ln_beta': _L0_xattn_in['ln_beta'], 'L0_ffn_gate_w': _L0_ffn_in['gate_w'], 'L0_ffn_gate_up_proj': _L0_ffn_in['gate_up_proj'], 'L0_ffn_down_proj': _L0_ffn_in['down_proj'], 'L0_ffn_shared_gate_w': _L0_ffn_in['shared_gate_w'], 'L0_ffn_shared_up_w': _L0_ffn_in['shared_up_w'], 'L0_ffn_shared_down_w': _L0_ffn_in['shared_down_w'], 'L0_ffn_shared_expert_gate_w': _L0_ffn_in['shared_expert_gate_w'], 'L1_xattn_Wc': _L1_xattn_in['Wc'], 'L1_xattn_bc': _L1_xattn_in['bc'], 'L1_ffn_gate_w': _L1_ffn_in['gate_w'], 'L1_ffn_gate_b': _L1_ffn_in['gate_b'], 'L1_ffn_w1': _L1_ffn_in['w1'], 'L1_ffn_b1': _L1_ffn_in['b1'], 'L1_ffn_w2': _L1_ffn_in['w2'], 'L1_ffn_b2': _L1_ffn_in['b2'], 'L1_ffn_w3': _L1_ffn_in['w3'], 'L1_ffn_b3': _L1_ffn_in['b3'], 'L1_ffn_ws1': _L1_ffn_in['ws1'], 'L1_ffn_bs1': _L1_ffn_in['bs1'], 'L1_ffn_ws2': _L1_ffn_in['ws2'], 'L1_ffn_bs2': _L1_ffn_in['bs2'], 'L1_ffn_ws3': _L1_ffn_in['ws3'], 'L1_ffn_bs3': _L1_ffn_in['bs3']}

def reference(x, ctx_512, g_xattn, g_ffn, L0_xattn_W_k, L0_xattn_b_k, L0_xattn_ln_gamma, L0_xattn_ln_beta, L0_ffn_gate_w, L0_ffn_gate_up_proj, L0_ffn_down_proj, L0_ffn_shared_gate_w, L0_ffn_shared_up_w, L0_ffn_shared_down_w, L0_ffn_shared_expert_gate_w, L1_xattn_Wc, L1_xattn_bc, L1_ffn_gate_w, L1_ffn_gate_b, L1_ffn_w1, L1_ffn_b1, L1_ffn_w2, L1_ffn_b2, L1_ffn_w3, L1_ffn_b3, L1_ffn_ws1, L1_ffn_bs1, L1_ffn_ws2, L1_ffn_bs2, L1_ffn_ws3, L1_ffn_bs3):
    import jax
    import jax.numpy as jnp

    def _L0_xattn_ref(p, k_v, W_k, b_k, ln_gamma, ln_beta):
        import jax, jax.numpy as jnp
        import numpy as np
        EPS = 1e-06
        IMAGE_DIMS = 512
        kv = k_v @ W_k.T + b_k
        out = jnp.einsum('bij,bjd->bid', p, kv)
        scale = IMAGE_DIMS ** (-0.5)
        sim = jnp.einsum('bid,bjd->bij', out, kv) * scale
        mu = jnp.mean(sim, axis=-1, keepdims=True)
        var = jnp.var(sim, axis=-1, keepdims=True)
        sim = (sim - mu) * jax.lax.rsqrt(var + EPS) * ln_gamma + ln_beta
        attn = jax.nn.softmax(sim, axis=-1)
        return attn

    def _L0_ffn_ref(hidden_states, gate_w, gate_up_proj, down_proj, shared_gate_w, shared_up_w, shared_down_w, shared_expert_gate_w):
        import jax, jax.numpy as jnp
        import numpy as np
        E = 8
        K = 2
        B, L, D = (2, 512, 512)
        I = 192
        IS = 1024
        Bb, Ll, Dd = hidden_states.shape
        h = hidden_states.reshape(-1, Dd)
        silu = jax.nn.silu
        shared = silu(h @ shared_gate_w.T) * (h @ shared_up_w.T) @ shared_down_w.T
        shared_out = jax.nn.sigmoid(h @ shared_expert_gate_w.T) * shared
        logits = h @ gate_w.T
        probs = jax.nn.softmax(logits, axis=-1)
        topk_w, topk_idx = jax.lax.top_k(probs, K)
        topk_w = topk_w / jnp.sum(topk_w, axis=-1, keepdims=True)
        cw = jnp.sum(jax.nn.one_hot(topk_idx, E, dtype=h.dtype) * topk_w[..., None], axis=1)
        gu = jnp.einsum('td,efd->tef', h, gate_up_proj)
        g, u = jnp.split(gu, 2, axis=-1)
        act = silu(g) * u
        out = jnp.einsum('tei,edi->ted', act, down_proj)
        partial = jnp.einsum('ted,te->td', out, cw)
        return (partial + shared_out).reshape(Bb, Ll, Dd)

    def _L1_xattn_ref(q, k, v, Wc, bc):
        import jax, jax.numpy as jnp
        import numpy as np
        import math
        D_MODEL = 512
        N_HEADS = 16
        N_GROUPS = 4
        HEADS_PER_GROUP = N_HEADS // N_GROUPS
        HEAD_DIM = D_MODEL // N_HEADS
        B, S = (2, 512)
        b, s, _ = q.shape
        qh = q.reshape(b, s, N_GROUPS, HEADS_PER_GROUP, HEAD_DIM).transpose(0, 2, 3, 1, 4)
        kh = k.reshape(b, s, N_GROUPS, HEAD_DIM).transpose(0, 2, 1, 3)
        vh = v.reshape(b, s, N_GROUPS, HEAD_DIM).transpose(0, 2, 1, 3)
        scale = 1.0 / math.sqrt(HEAD_DIM)
        scores = jnp.einsum('bghsd,bgtd->bghst', qh, kh) * scale
        probs = jax.nn.softmax(scores, axis=-1)
        out = jnp.einsum('bghst,bgtd->bghsd', probs, vh)
        out = out.transpose(0, 3, 1, 2, 4).reshape(b, s, D_MODEL)
        return out @ Wc.T + bc

    def _L1_ffn_ref(x, gate_w, gate_b, w1, b1, w2, b2, w3, b3, ws1, bs1, ws2, bs2, ws3, bs3):
        import jax, jax.numpy as jnp
        import numpy as np
        E = 16
        D = 512
        H = 352
        HS = 2 * 352
        TOP_K = 6
        ROUTE_SCALE = 1.0
        shape = x.shape
        xf = x.reshape(-1, shape[-1])
        scores = xf @ gate_w.T
        probs = jax.nn.softmax(scores.astype(jnp.float32), axis=-1)
        biased = probs + gate_b
        _, idx = jax.lax.top_k(biased, TOP_K)
        weights = jnp.take_along_axis(probs, idx, axis=1) * ROUTE_SCALE
        weights = weights.astype(x.dtype)
        onehot = jax.nn.one_hot(idx, E, dtype=weights.dtype)
        cw = jnp.einsum('tk,tke->te', weights, onehot)

        def expert_step(y, params):
            W1, B1, W2, B2, W3, B3, c = params
            h = jax.nn.silu(xf @ W1.T + B1) * (xf @ W3.T + B3)
            out = h @ W2.T + B2
            return (y + c[:, None] * out, None)
        y0 = jnp.zeros_like(xf)
        y, _ = jax.lax.scan(expert_step, y0, (w1, b1, w2, b2, w3, b3, cw.T))
        z = jax.nn.silu(xf @ ws1.T + bs1) * (xf @ ws3.T + bs3) @ ws2.T + bs2
        return (y + z).reshape(shape)
    x = x + jnp.tanh(g_xattn[0]) * _L0_xattn_ref(_layernorm(x, axis=-1), ctx_512, L0_xattn_W_k, L0_xattn_b_k, L0_xattn_ln_gamma, L0_xattn_ln_beta)
    x = x + jnp.tanh(g_ffn[0]) * _L0_ffn_ref(_layernorm(x, axis=-1), L0_ffn_gate_w, L0_ffn_gate_up_proj, L0_ffn_down_proj, L0_ffn_shared_gate_w, L0_ffn_shared_up_w, L0_ffn_shared_down_w, L0_ffn_shared_expert_gate_w)
    x = x + jnp.tanh(g_xattn[1]) * _L1_xattn_ref(_layernorm(x, axis=-1), ctx_512, ctx_512, L1_xattn_Wc, L1_xattn_bc)
    x = x + jnp.tanh(g_ffn[1]) * _L1_ffn_ref(_layernorm(x, axis=-1), L1_ffn_gate_w, L1_ffn_gate_b, L1_ffn_w1, L1_ffn_b1, L1_ffn_w2, L1_ffn_b2, L1_ffn_w3, L1_ffn_b3, L1_ffn_ws1, L1_ffn_bs1, L1_ffn_ws2, L1_ffn_bs2, L1_ffn_ws3, L1_ffn_bs3)
    return x

_drawn_inputs = setup_inputs


def setup_inputs(seed=0):
    import zlib

    import numpy as np

    out = dict(_drawn_inputs(seed))
    spreads = {'g_ffn': (-1.0, 0.6),
     'L0_xattn_b_k': (0.0, 2.0),
     'L0_xattn_ln_gamma': (1.0, 0.6),
     'L0_xattn_ln_beta': (0.0, 0.8)}
    factors = {'L0_xattn_W_k': 8.0,
     'L0_ffn_gate_w': 4.147,
     'L0_ffn_gate_up_proj': 3.549,
     'L0_ffn_down_proj': 3.563,
     'L0_ffn_shared_expert_gate_w': 8.0,
     'L1_ffn_gate_w': 8.0,
     'L1_ffn_gate_b': 8.0,
     'L1_ffn_w1': 7.542,
     'L1_ffn_b1': 28.198,
     'L1_ffn_w2': 7.299,
     'L1_ffn_b2': 180.846,
     'L1_ffn_w3': 7.31,
     'L1_ffn_b3': 28.156,
     'L1_ffn_bs1': 64.0,
     'L1_ffn_bs2': 134.105,
     'L1_ffn_bs3': 64.0,
     'L1_ffn_ws1': 8.0,
     'L1_ffn_ws2': 8.0,
     'L1_ffn_ws3': 8.0}
    for name, (base, spread) in spreads.items():
        noise = np.random.default_rng([zlib.crc32(name.encode()), seed]).standard_normal(out[name].shape)
        drawn = base * np.exp(spread * noise) if base else spread * noise
        out[name] = jnp.asarray(drawn.astype(out[name].dtype))
    for name, factor in factors.items():
        out[name] = (out[name] * factor).astype(out[name].dtype)
    return out
```

```python
from contextlib import ExitStack

import numpy as np
import concourse.bass as bass
from concourse import mybir

F32 = mybir.dt.float32
F32R = mybir.dt.float32r
BF16 = mybir.dt.bfloat16
F16 = mybir.dt.float16
ALU = mybir.AluOpType
ACT = mybir.ActivationFunctionType
AX = mybir.AxisListType

P = 128
B, S, D = 4, 512, 512
NT = B * S // P
TB = S // P
KD = D // P
DC = 128
HEADS, GROUPS, HD = 16, 4, 32
HPG = HEADS // GROUPS
LN_EPS = 1e-5
SIM_EPS = 1e-6
SIM_SCALE = float(S) ** -0.5
ATT_SCALE = float(HD) ** -0.5
BIAS_ROW = 64
STRIPS = 4

MOE = [
    dict(E=8, K=2, H=192, HS=1024, gates=9, slots=3, biased=False,
         loops=[(6, (0, 1)), (4, (2, 2))]),
    dict(E=16, K=6, H=352, HS=704, gates=16, slots=4, biased=True,
         loops=[(11, (0, 1)), (11, (2, 3)), (2, None), (1, (None, "last"))]),
]
for m in MOE:
    m["pairs"] = sum(n for n, _ in m["loops"])


def flt(ap):
    return ap.bitcast(F32)


def build(nc, a):
    x_d = a["x"].rearrange("b (t p) d -> p (b t) d", p=P)
    out_d = a["out"].rearrange("b (t p) d -> p (b t) d", p=P)

    with ExitStack() as ctx:
        def sb(stack, name, shape, dt=F32):
            return stack.enter_context(nc.sbuf_tensor(name, shape, dt))

        x = sb(ctx, "x_res", [P, NT, D])
        ident = sb(ctx, "ident", [P, P])
        gates = sb(ctx, "gates", [P, 4])
        stats = sb(ctx, "stats", [P, NT, 6])
        eps = sb(ctx, "eps", [P, 2])
        msum = sb(ctx, "msum", [P, TB])
        mdif = sb(ctx, "mdif", [P, TB])
        vraw = sb(ctx, "vraw", [P, TB])
        std = sb(ctx, "std", [P, TB])
        inv = sb(ctx, "inv", [P, TB])
        rstd = sb(ctx, "rstd", [P, NT])
        nbias = sb(ctx, "nbias", [P, NT])
        xn = sb(ctx, "xn", [P, TB, D])
        ps = ctx.enter_context(nc.psum_tensor("ps", [P, 8, 512], F32))

        s_stats, s_small, s_var, s_std, s_ln = (
            ctx.enter_context(nc.semaphore(n)) for n in ("ln_stats", "ln_small", "ln_var", "ln_std", "ln_ready"))

        def row_stats(dve, nth, b):
            n = B * nth + b
            at = bass.ds(TB * b, TB)
            for t in range(TB):
                dve.bn_stats(stats[:, bass.ds(TB * b + t, 1), :], x[:, bass.ds(TB * b + t, 1), :]).then_inc(s_stats, 1)
            dve.wait_ge(s_stats, TB * n + TB)
            dve.tensor_tensor(msum[:], stats[:, at, 1], stats[:, at, 4], ALU.add)
            dve.tensor_tensor(mdif[:], stats[:, at, 1], stats[:, at, 4], ALU.subtract)
            dve.tensor_tensor(vraw[:], stats[:, at, 2], stats[:, at, 5], ALU.add).then_inc(s_small, 1)
            dve.wait_ge(s_small, 3 * n + 1)
            dve.tensor_tensor(mdif[:], mdif[:], mdif[:], ALU.mult).then_inc(s_small, 1)
            dve.wait_ge(s_small, 3 * n + 2)
            dve.scalar_tensor_tensor(out=vraw[:], in0=mdif[:], scalar=D / 4.0, in1=vraw[:],
                                     op0=ALU.mult, op1=ALU.add).then_inc(s_var, 1)
            dve.wait_ge(s_std, n + 1)
            dve.reciprocal(inv[:], std[:]).then_inc(s_small, 1)
            dve.wait_ge(s_small, 3 * n + 3)
            dve.tensor_scalar(rstd[:, at], inv[:], 1.0, None, ALU.mult)
            dve.scalar_tensor_tensor(out=nbias[:, at], in0=msum[:], scalar=-0.5, in1=inv[:],
                                     op0=ALU.mult, op1=ALU.mult).then_inc(s_ln, 1)
            dve.wait_ge(s_ln, n + 1)

        def deviation(act, nth, b):
            act.wait_ge(s_var, B * nth + b + 1)
            act.activation(std[:], vraw[:], ACT.Sqrt, scale=1.0 / D, bias=eps[:, 0:1]).then_inc(s_std, 1)

        def normalise(act, t, T, nth, s_xn):
            act.wait_ge(s_ln, B * nth + 1)
            act.activation(xn[:, t, :], x[:, T, :], ACT.Identity, scale=rstd[:, bass.ds(T, 1)],
                           bias=nbias[:, bass.ds(T, 1)]).then_inc(s_xn, 1)

        cross_attention_0(nc, a, sb, locals())
        for layer in range(2):
            if layer == 1:
                cross_attention_1(nc, a, sb, locals())
            mixture(nc, a, sb, locals(), layer)


def cross_attention_0(nc, a, sb, g):
    x, ident, gates, eps, xn, ps = (g[k] for k in ("x", "ident", "gates", "eps", "xn", "ps"))
    with ExitStack() as ctx:
        ctxT = sb(ctx, "a0_ctxT", [P, B, S])
        wkT = sb(ctx, "a0_wkT", [P, DC])
        bk = sb(ctx, "a0_bk", [P, 1])
        gamma = sb(ctx, "a0_gamma", [P, S])
        beta = sb(ctx, "a0_beta", [P, S])
        graw = sb(ctx, "a0_graw", [P, 4])
        kvT = sb(ctx, "a0_kvT", [P, S])
        kv = sb(ctx, "a0_kv", [P, TB, DC])
        pT = sb(ctx, "a0_pT", [P, KD, S])
        oT = sb(ctx, "a0_oT", [P, S])
        y = sb(ctx, "a0_y", [P, TB, S])
        st = sb(ctx, "a0_st", [P, TB, 6])
        m_sum = sb(ctx, "a0_msum", [P, TB])
        m_dif = sb(ctx, "a0_mdif", [P, TB])
        v_raw = sb(ctx, "a0_vraw", [P, TB])
        s_dev = sb(ctx, "a0_sdev", [P, TB])
        r_std = sb(ctx, "a0_rstd", [P, TB])
        n_bias = sb(ctx, "a0_nbias", [P, TB])
        mx = sb(ctx, "a0_mx", [P, TB])
        nmx = sb(ctx, "a0_nmx", [P, TB])
        den = sb(ctx, "a0_den", [P, TB])
        rden = sb(ctx, "a0_rden", [P, TB])
        coef = sb(ctx, "a0_coef", [P, TB])

        def sem(name):
            return ctx.enter_context(nc.semaphore("a0_" + name))

        x_in, par_in = [sem(f"x_in{b}") for b in range(B)], sem("par_in")
        gates_ready, gamma_done = sem("gates"), sem("gamma_done")
        xn_ready, xn_read = sem("xn"), sem("xn_read")
        kvT_mm, kvT_ready, kv_tr, kv_ready = sem("kvT_mm"), sem("kvT"), sem("kv_tr"), sem("kv")
        pT_ready, oT_mm, oT_ready = sem("pT"), sem("oT_mm"), sem("oT")
        sim_ready, sim_used = sem("sim"), sem("sim_used")
        eps_set = sem("eps_set")
        st_done, chain, svar, sdev_ready = sem("st"), sem("chain"), sem("svar"), sem("sdev")
        scaled, nmx_ready, exp_done, x_new = sem("scaled"), sem("nmx"), sem("exp"), sem("x_new")

        with nc.Block() as block:
            @block.sync
            def _(sp):
                for b in range(B):
                    sp.dma_start(x[:, TB * b:TB * b + TB, :],
                                 g["x_d"][:, TB * b:TB * b + TB, :]).then_inc(x_in[b], 16)
                sp.dma_start(ident[:], a["ident"]).then_inc(par_in, 16)
                sp.dma_start(wkT[:], a["a0_wT"]).then_inc(par_in, 16)
                sp.dma_start(ctxT[:], a["ctxT"].rearrange("b d s -> d b s")).then_inc(par_in, 16)
                sp.dma_start(bk[:], a["a0_b"]).then_inc(par_in, 16)
                sp.dma_start(gamma[:], a["a0_gamma"].to_broadcast([P, S])).then_inc(par_in, 16)
                sp.dma_start(beta[:], a["a0_beta"].to_broadcast([P, S])).then_inc(par_in, 16)
                sp.dma_start(graw[:, 0:2], a["g_xattn"].to_broadcast([P, 2])).then_inc(par_in, 16)
                sp.dma_start(graw[:, 2:4], a["g_ffn"].to_broadcast([P, 2])).then_inc(par_in, 16)

            PARAMS = 16 * 8

            @block.gpsimd
            def _(pool):
                pool.memset(eps[:, 0:1], LN_EPS)
                pool.memset(eps[:, 1:2], SIM_EPS).then_inc(eps_set, 1)

            def prepare_scalar(act, b):
                act.wait_ge(g["s_ln"], b + 1)
                for t in range(TB):
                    act.wait_ge(xn_read, TB * b + t + 1)
                    g["normalise"](act, t, TB * b + t, 0, xn_ready)
                act.wait_ge(kvT_mm, b + 1)
                act.wait_ge(sim_ready, TB * b + TB)
                act.activation(kvT[:], ps[:, 4, :], ACT.Identity, bias=bk[:, 0:1]).then_inc(kvT_ready, 1)
                act.wait_ge(kv_tr, b + 1)
                act.copy(kv[:].rearrange("p t d -> p (t d)"), ps[:, 5, :]).then_inc(kv_ready, 1)
                act.wait_ge(xn_read, TB * b + 2 * TB)
                for k in range(KD):
                    act.copy(pT[:, k, :], ps[:, 4 + k, :]).then_inc(pT_ready, 1)
                act.wait_ge(oT_mm, b + 1)
                act.mul(oT[:], ps[:, 4, :], SIM_SCALE).then_inc(oT_ready, 1)

            def finish_scalar(act, b):
                act.wait_ge(svar, b + 1)
                act.activation(s_dev[:], v_raw[:], ACT.Sqrt, scale=1.0 / S, bias=eps[:, 1:2]).then_inc(sdev_ready, 1)
                for t in range(TB):
                    act.wait_ge(nmx_ready, TB * b + t + 1)
                    act.activation(y[:, t, :], y[:, t, :], ACT.Exp, bias=nmx[:, t:t + 1],
                                   accum_out=den[:, t:t + 1]).then_inc(exp_done, 1)

            @block.scalar
            def _(act):
                act.wait_ge(eps_set, 1)
                g["deviation"](act, 0, 0)
                act.wait_ge(par_in, PARAMS)
                act.activation(gates[:], graw[:], ACT.Tanh).then_inc(gates_ready, 1)
                prepare_scalar(act, 0)
                for b in range(1, B):
                    g["deviation"](act, 0, b)
                with act.Fori(0, B - 1) as b:
                    prepare_scalar(act, b + 1)
                    finish_scalar(act, b)
                finish_scalar(act, B - 1)

            @block.tensor
            def _(pe):
                pe.sem_inc(xn_read, TB)
                pe.sem_inc(sim_ready, TB)
                pe.wait_ge(par_in, PARAMS)
                with pe.Fori(0, B) as b:
                    pe.matmul(ps[:, 4, :], wkT[:], ctxT[:, b, :], start=True, stop=True).then_inc(kvT_mm, 1)
                    pe.wait_ge(kvT_ready, b + 1)
                    for c in range(TB):
                        mm = pe.transpose(ps[:, 5, P * c:P * c + P], kvT[:, P * c:P * c + P], ident[:])
                    mm.then_inc(kv_tr, 1)
                    pe.wait_ge(kv_ready, b + 1)
                    for t in range(TB):
                        pe.wait_ge(xn_ready, TB * b + t + 1)
                        for k in range(KD):
                            mm = pe.transpose(ps[:, 4 + k, P * t:P * t + P], xn[:, t, P * k:P * k + P], ident[:])
                        mm.then_inc(xn_read, 1)
                    pe.wait_ge(pT_ready, KD * b + KD)
                    for k in range(KD):
                        mm = pe.matmul(ps[:, 4, :], kv[:, k, :], pT[:, k, :], start=(k == 0), stop=(k == KD - 1))
                    mm.then_inc(oT_mm, 1)
                    pe.wait_ge(oT_ready, b + 1)
                    for t in range(TB):
                        pe.wait_ge(sim_used, TB * b + t + 1)
                        pe.matmul(ps[:, t, :], oT[:, P * t:P * t + P], kvT[:], start=True,
                                  stop=True).then_inc(sim_ready, 1)

            @block.vector
            def _(dve):
                dve.sem_inc(sim_used, TB)
                for b in range(B):
                    dve.wait_ge(x_in[b], 16)
                    g["row_stats"](dve, 0, b)
                dve.wait_ge(par_in, PARAMS)
                dve.wait_ge(gates_ready, 1)
                with dve.Fori(0, B) as b:
                    for t in range(TB):
                        dve.wait_ge(sim_ready, TB * b + TB + t + 1)
                        dve.bn_stats(st[:, t, :], ps[:, t, :]).then_inc(st_done, 1)
                    dve.wait_ge(st_done, TB * b + TB)
                    dve.tensor_tensor(m_sum[:], st[:, :, 1], st[:, :, 4], ALU.add)
                    dve.tensor_tensor(m_dif[:], st[:, :, 1], st[:, :, 4], ALU.subtract)
                    dve.tensor_tensor(v_raw[:], st[:, :, 2], st[:, :, 5], ALU.add).then_inc(chain, 1)
                    dve.wait_ge(chain, 6 * b + 1)
                    dve.tensor_tensor(m_dif[:], m_dif[:], m_dif[:], ALU.mult).then_inc(chain, 1)
                    dve.wait_ge(chain, 6 * b + 2)
                    dve.scalar_tensor_tensor(out=v_raw[:], in0=m_dif[:], scalar=S / 4.0, in1=v_raw[:],
                                             op0=ALU.mult, op1=ALU.add).then_inc(svar, 1)
                    dve.wait_ge(sdev_ready, b + 1)
                    dve.reciprocal(r_std[:], s_dev[:]).then_inc(chain, 1)
                    dve.wait_ge(chain, 6 * b + 3)
                    dve.scalar_tensor_tensor(out=n_bias[:], in0=m_sum[:], scalar=-0.5, in1=r_std[:],
                                             op0=ALU.mult, op1=ALU.mult).then_inc(chain, 1)
                    dve.wait_ge(chain, 6 * b + 4)
                    for t in range(TB):
                        dve.tensor_scalar(y[:, t, :], ps[:, t, :], r_std[:, t:t + 1], n_bias[:, t:t + 1],
                                          ALU.mult, ALU.add).then_inc(sim_used, 1)
                    for t in range(TB):
                        dve.wait_ge(sim_used, TB * b + TB + t + 1)
                        dve.tensor_tensor(y[:, t, :], y[:, t, :], gamma[:], ALU.mult).then_inc(scaled, 1)
                    dve.wait_ge(scaled, 2 * TB * b + TB)
                    dve.sem_inc(gamma_done, 1)
                    for t in range(TB):
                        dve.tensor_tensor_reduce(y[:, t, :], y[:, t, :], beta[:], 1.0, -3.0e38, ALU.add,
                                                 ALU.max, mx[:, t:t + 1]).then_inc(scaled, 1)
                    for t in range(TB):
                        dve.wait_ge(scaled, 2 * TB * b + TB + t + 1)
                        dve.tensor_scalar(nmx[:, t:t + 1], mx[:, t:t + 1], -1.0, None,
                                          ALU.mult).then_inc(nmx_ready, 1)
                    dve.wait_ge(exp_done, TB * b + TB)
                    dve.reciprocal(rden[:], den[:]).then_inc(chain, 1)
                    dve.wait_ge(chain, 6 * b + 5)
                    dve.tensor_scalar(coef[:], rden[:], gates[:, 0:1], None, ALU.mult).then_inc(chain, 1)
                    dve.wait_ge(chain, 6 * b + 6)
                    for t in range(TB):
                        dve.scalar_tensor_tensor(out=x[:, TB * b + t, :], in0=y[:, t, :], scalar=coef[:, t:t + 1],
                                                 in1=x[:, TB * b + t, :], op0=ALU.mult,
                                                 op1=ALU.add).then_inc(x_new, 1)
                    dve.wait_ge(x_new, TB * b + TB)


def cross_attention_1(nc, a, sb, g):
    x, ident, gates, rstd, nbias, ps = (g[k] for k in ("x", "ident", "gates", "rstd", "nbias", "ps"))
    UNITS = B * GROUPS
    VC = 3 * HD + 1
    A_BANK, PV_BANK, MISC = 4, 6, 7
    CUT = 256
    with ExitStack() as ctx:
        qs = sb(ctx, "a1_qs", [P, HEADS, S], F32R)
        ks = sb(ctx, "a1_ks", [P, GROUPS, S], F32R)
        kraw = sb(ctx, "a1_kraw", [3 * HD, 2, S])
        xc = sb(ctx, "a1_xc", [P, 2, TB, P])
        qhi = sb(ctx, "a1_qhi", [P, 2, S], F32R)
        qlo = sb(ctx, "a1_qlo", [P, 2, S], F32R)
        vraw = sb(ctx, "a1_vraw", [P, NT, DC])
        vres = sb(ctx, "a1_vres", [P, TB, DC])
        v3 = sb(ctx, "a1_v3", [P, NT, GROUPS, VC + 1], BF16)
        nmax = sb(ctx, "a1_nmax", [P, 2, HPG * TB])
        mhi = sb(ctx, "a1_mhi", [HPG * TB, 2, P], F32R)
        mlo = sb(ctx, "a1_mlo", [HPG * TB, 2, P], F32R)
        e32 = sb(ctx, "a1_e32", [P, 2, 2, S])
        ehi = sb(ctx, "a1_ehi", [P, 4, 2, S], F16)
        elo = sb(ctx, "a1_elo", [P, 4, 2, S], F16)
        osum = sb(ctx, "a1_osum", [P, TB, HD])
        rden = sb(ctx, "a1_rden", [P, TB])
        otok = sb(ctx, "a1_otok", [P, TB, D])
        oT = sb(ctx, "a1_oT", [P, TB, GROUPS, P])
        wcT = sb(ctx, "a1_wcT", [P, KD, D])
        bc = sb(ctx, "a1_bc", [P, D])
        t_out = sb(ctx, "a1_tout", [P, D])

        def sem(name):
            return ctx.enter_context(nc.semaphore("a1_" + name))

        par_in, zero_set = sem("par_in"), sem("zero")
        v_in = sem("v_in")
        k_in, strips_in, m_in = ([sem(f"{n}{i}") for i in range(2)] for n in ("k_in", "strips_in", "m_in"))
        xc_free, scaled, xc_ready, q_tr, qhi_ready, qlo_ready = (
            sem(n) for n in ("xc_free", "scaled", "xc", "q_tr", "qhi", "qlo"))
        khi_ready, klo_ready, v_step, v_ready = sem("khi"), sem("klo"), sem("v_step"), sem("v")
        raw_ready, max_done, max_tr, mhi_ready, mlo_ready = (
            sem(n) for n in ("raw", "max", "max_tr", "mhi", "mlo"))
        sc_ready, e32_done, exp_done, lo_dve, lo_pool, pv_done = (
            sem(n) for n in ("sc", "e32", "exp", "lo_dve", "lo_pool", "pv"))
        rden_ready, sum_ready, o_ready = sem("rden"), sem("osum"), sem("o")
        o_tr, oT_ready, wc_done, wc_used, x_new = (sem(n) for n in ("o_tr", "oT", "wc", "wc_used", "x_new"))

        def wait(eng, s, value):
            if not isinstance(value, int) or value > 0:
                eng.wait_ge(s, value)

        def turn(u, grp):
            return (u - grp % 2) // 2 + 1

        def ahead(u, grp, j, has_prepare, has_maxima):
            if j < 4:
                return (u + 1, (grp + 1) % GROUPS, range(2 * j + 8, 2 * j + 10)) if has_maxima else (0, 0, ())
            return (u + 2, (grp + 2) % GROUPS, range(2 * j - 8, 2 * j - 6)) if has_prepare else (0, 0, ())

        JOBS = {(2, 6): ("turn", 0, 0), (3, 2): ("turn", 0, 1), (3, 6): ("turn", 0, 2), (0, 2): ("turn", 1, 3),
                (0, 6): ("tile", 1, 0), (1, 2): ("tile", 1, 1), (1, 6): ("tile", 1, 2), (2, 2): ("tile", 1, 3)}

        def job(grp, j, b):
            kind, back, number = JOBS.get((grp, j), (None, 0, 0))
            return None if kind is None or (isinstance(b, int) and b < back) else (kind, b - back, number)

        def last_job(grp, b):
            return job(grp - 1, 6, b) if grp > 0 else None if isinstance(b, int) and b < 1 else job(3, 6, b - 1)

        def batches(eng, unit):
            for grp in range(GROUPS):
                unit(grp, grp, True, True, None)
            with eng.Fori(1, B - 1) as b:
                for grp in range(GROUPS):
                    unit(GROUPS * b + grp, grp, True, True, b - 1)
            for grp in range(GROUPS):
                u = GROUPS * (B - 1) + grp
                unit(u, grp, u + 2 < UNITS, u + 1 < UNITS, B - 2)

        with nc.Block() as block:
            @block.sync
            def _(sp):
                sp.dma_start(wcT[:], a["a1_wcT"].rearrange("(k p) n -> p k n", p=P)).then_inc(par_in, 16)
                sp.dma_start(bc[:], a["a1_bc"].to_broadcast([P, D])).then_inc(par_in, 16)
                kT_d = a["ctxT"].rearrange("b (g d) s -> (b g) d s", g=GROUPS)
                for b in range(B):
                    sp.dma_start(vraw[:, TB * b:TB * b + TB, :],
                                 a["ctx_512"][b, :, :].rearrange("(t p) d -> p t d", p=P)).then_inc(v_in, 16)

                def load(u, grp):
                    wait(sp, klo_ready, u - 1)
                    for i in range(3):
                        sp.dma_start(kraw[HD * i:HD * i + HD, grp % 2, :],
                                     kT_d[bass.ds(u, 1), :, :].rearrange("o d s -> d (o s)")
                                     ).then_inc(k_in[grp % 2], 16)

                def strips(u, grp):
                    sp.wait_ge(qhi_ready, u + 1)
                    heads = slice(HPG * grp, HPG * grp + HPG)
                    for i in range(2):
                        sp.dma_start(flt(qs[HD * i:HD * i + HD, heads, :]),
                                     flt(qhi[:, grp % 2, :])).then_inc(strips_in[grp % 2], 16)
                    sp.wait_ge(qlo_ready, u + 1)
                    sp.dma_start(flt(qs[2 * HD:3 * HD, heads, :]),
                                 flt(qlo[:, grp % 2, :])).then_inc(strips_in[grp % 2], 16)

                def maxima(u, grp):
                    sp.wait_ge(mlo_ready, u + 1)
                    for i, m in enumerate((mhi, mlo)):
                        sp.dma_start(flt(qs[3 * HD + i:3 * HD + i + 1, HPG * grp:HPG * grp + HPG, :]),
                                     flt(m[:, grp % 2, :])).then_inc(m_in[grp % 2], 16)

                load(0, 0)
                load(1, 1)
                strips(0, 0)
                strips(1, 1)
                maxima(0, 0)

                def unit(u, grp, has_prepare, has_maxima, wc_batch):
                    if has_prepare:
                        load(u + 2, (grp + 2) % GROUPS)
                        strips(u + 2, (grp + 2) % GROUPS)
                    if has_maxima:
                        maxima(u + 1, (grp + 1) % GROUPS)

                batches(sp, unit)

            def prepare_pool(pool, u, grp, b):
                wait(pool, q_tr, u - 1)
                pool.sem_inc(xc_free, 1)
                wide = [P, TB, P]
                pool.tensor_tensor(xc[:, grp % 2, :, :].rearrange("p t (d q) -> p t d q", q=HPG),
                                   x[:, bass.ds(TB * b, TB), P * grp:P * grp + P]
                                   .rearrange("p t (q d) -> p t d q", q=HPG),
                                   rstd[:, bass.ds(TB * b, TB)].unsqueeze(2).unsqueeze(3)
                                   .to_broadcast([P, TB, HD, HPG]),
                                   ALU.mult).then_inc(scaled, 1)
                pool.wait_ge(scaled, u + 1)
                pool.sem_inc(xc_free, 1)
                pool.tensor_tensor(xc[:, grp % 2, :, :], xc[:, grp % 2, :, :],
                                   nbias[:, bass.ds(TB * b, TB)].unsqueeze(2).to_broadcast(wide),
                                   ALU.add).then_inc(xc_ready, 1)

            def keys_pool(pool, u, grp):
                pool.wait_ge(khi_ready, u + 1)
                pool.tensor_tensor(ks[HD:2 * HD, grp, :], kraw[HD:2 * HD, grp % 2, :], flt(ks[HD:2 * HD, grp, :]),
                                   ALU.subtract).then_inc(klo_ready, 1)
                pool.wait_ge(klo_ready, u + 1)

            def values_pool(pool, b):
                rows = slice(TB * b, TB * b + TB)
                raw = vraw[:, rows, :].rearrange("p t (g d) -> p t g d", g=GROUPS)
                res = vres[:].rearrange("p t (g d) -> p t g d", g=GROUPS)
                hi, mid, lo = (v3[:, rows, :, HD * i:HD * i + HD] for i in range(3))
                pool.wait_ge(v_in, 16 * B)
                if b > 0:
                    pool.wait_ge(v_ready, b)
                pool.tensor_copy(hi, raw).then_inc(v_step, 1)
                pool.wait_ge(v_step, 3 * b + 1)
                pool.tensor_tensor(res, raw, hi, ALU.subtract).then_inc(v_step, 1)
                pool.wait_ge(v_step, 3 * b + 2)
                pool.tensor_copy(mid, res).then_inc(v_step, 1)
                pool.wait_ge(v_step, 3 * b + 3)
                pool.tensor_tensor(lo, res, mid, ALU.subtract).then_inc(v_ready, 1)

            @block.gpsimd
            def _(pool):
                pool.memset(flt(ks[3 * HD:3 * HD + 2, :, :]), 1.0).then_inc(zero_set, 1)
                pool.wait_ge(zero_set, 1)
                pool.memset(v3[:, :, :, 3 * HD:3 * HD + 2], 1.0).then_inc(zero_set, 1)
                pool.wait_ge(zero_set, 2)
                keys_pool(pool, 0, 0)
                keys_pool(pool, 1, 1)
                values_pool(pool, 0)
                pool.wait_ge(g["s_ln"], 2 * B + 1)
                for u in range(3):
                    prepare_pool(pool, u, u, 0)
                for b in range(1, B):
                    values_pool(pool, b)
                pool.wait_ge(g["s_ln"], 2 * B + B)

                def unit(u, grp, has_prepare, has_maxima, wc_batch):
                    has_columns = has_prepare and not (isinstance(u, int) and u + 3 == UNITS)
                    for j in range(8):
                        n = 8 * u + j
                        pool.wait_ge(exp_done, n + 1)
                        e, h, l = (m.rearrange("p i s -> p (i s)")[:, CUT:] for m in
                                   (e32[:, j % 2, :, :], ehi[:, j % 4, :, :], elo[:, j % 4, :, :]))
                        pool.tensor_tensor(l, e, h, ALU.subtract).then_inc(lo_pool, 1)
                        if j == 5 and has_columns:
                            b3 = (0 if wc_batch is None else wc_batch + 1) + (grp + 3) // GROUPS
                            prepare_pool(pool, u + 3, (grp + 3) % GROUPS, b3)
                        if j == 1 and has_prepare:
                            pool.wait_ge(lo_pool, n + 1)
                            keys_pool(pool, u + 2, (grp + 2) % GROUPS)

                batches(pool, unit)

            def keys_scalar(act, u, grp):
                act.wait_ge(k_in[grp % 2], 48 * turn(u, grp))
                act.copy(ks[0:3 * HD, grp, :], kraw[:, grp % 2, :]).then_inc(khi_ready, 1)

            def prepare_scalar(act, u, grp):
                act.wait_ge(q_tr, u + 1)
                wait(act, strips_in[grp % 2], 48 * (turn(u, grp) - 1))
                act.mul(qhi[:, grp % 2, :], ps[:, MISC, :], ATT_SCALE).then_inc(qhi_ready, 1)

            def maxima_scalar(act, u, grp):
                act.wait_ge(max_tr, u + 1)
                wait(act, m_in[grp % 2], 32 * (turn(u, grp) - 1))
                act.copy(mhi[:, grp % 2, :], ps[0:HPG * TB, MISC, 0:P]).then_inc(mhi_ready, 1)

            def turn_scalar(act, b, k):
                act.wait_ge(o_tr, GROUPS * b + k + 1)
                act.copy(oT[:, :, k, :], ps[:, MISC, :].rearrange("p (t s) -> p t s", t=TB)).then_inc(oT_ready, 1)

            @block.scalar
            def _(act):
                keys_scalar(act, 0, 0)
                keys_scalar(act, 1, 1)
                for b in range(B):
                    g["deviation"](act, 2, b)
                prepare_scalar(act, 0, 0)
                prepare_scalar(act, 1, 1)
                maxima_scalar(act, 0, 0)

                def unit(u, grp, has_prepare, has_maxima, wc_batch):
                    b = 0 if wc_batch is None else wc_batch + 1
                    for j in range(8):
                        n = 8 * u + j
                        wait(act, lo_dve, n - 1)
                        wait(act, lo_pool, n - 1)
                        act.wait_ge(sc_ready, n + 1)
                        act.activation(e32[:, j % 2, :, :], ps[:, 2 * (j % 2):2 * (j % 2) + 2, :],
                                       ACT.Exp).then_inc(e32_done, 1)
                        wait(act, pv_done, n - 3)
                        act.activation(ehi[:, j % 4, :, :], ps[:, 2 * (j % 2):2 * (j % 2) + 2, :],
                                       ACT.Exp).then_inc(exp_done, 1)
                        if j in (3, 7) and job(grp, j - 1, b) and job(grp, j - 1, b)[0] == "turn":
                            turn_scalar(act, *job(grp, j - 1, b)[1:])
                        if j == 0 and has_prepare:
                            keys_scalar(act, u + 2, (grp + 2) % GROUPS)
                        if j == 1 and has_prepare:
                            prepare_scalar(act, u + 2, (grp + 2) % GROUPS)
                        if j == 5 and has_maxima:
                            maxima_scalar(act, u + 1, (grp + 1) % GROUPS)

                batches(act, unit)
                turn_scalar(act, B - 1, GROUPS - 1)

            def prepare_tensor(pe, u, grp):
                pe.wait_ge(xc_ready, u + 1)
                for t in range(TB):
                    mm = pe.transpose(ps[:, MISC, P * t:P * t + P], xc[:, grp % 2, t, :], ident[:])
                mm.then_inc(q_tr, 1)

            def raw_tensor(pe, u, grp, steps):
                for n in steps:
                    q, t = n // TB, n % TB
                    if n == 0:
                        pe.wait_ge(strips_in[grp % 2], 48 * turn(u, grp))
                        pe.wait_ge(klo_ready, u + 1)
                    wait(pe, max_done, 16 * u + n - 1)
                    pe.matmul(ps[:, A_BANK + n % 2, :], qs[0:3 * HD, HPG * grp + q, P * t:P * t + P],
                              ks[0:3 * HD, grp, :], start=True, stop=True).then_inc(raw_ready, 1)

            def maxima_tensor(pe, u, grp):
                pe.wait_ge(max_done, 16 * u + 16)
                pe.transpose(ps[0:HPG * TB, MISC, 0:P], nmax[:, grp % 2, :], ident[:]).then_inc(max_tr, 1)

            def scores_tensor(pe, u, grp, j):
                n = 8 * u + j
                if j == 0:
                    pe.wait_ge(m_in[grp % 2], 32 * turn(u, grp))
                wait(pe, exp_done, n - 1)
                for i in range(2):
                    c = 2 * (j % 2) + i
                    mm = pe.matmul(ps[:, 2 * (j % 2) + i, :], ks[0:3 * HD + 2, grp, P * c:P * c + P],
                                   qs[0:3 * HD + 2, HPG * grp + j // 2, :], start=True, stop=True)
                mm.then_inc(sc_ready, 1)

            def pv_tensor(pe, u, grp, j, b):
                n = 8 * u + j
                if j % 2 == 0:
                    wait(pe, sum_ready, 4 * u + j // 2)
                pe.wait_ge(lo_dve, n + 1)
                pe.wait_ge(lo_pool, n + 1)
                for t in range(TB):
                    for i in range(2):
                        for part in (ehi, elo):
                            mm = pe.matmul(ps[:, PV_BANK, P * t:P * t + VC], part[:, j % 4, i, P * t:P * t + P],
                                           v3[:, bass.ds(TB * b + 2 * (j % 2) + i, 1), grp, 0:VC],
                                           start=(j % 2 == 0 and t == 0 and i == 0 and part is ehi),
                                           stop=(j % 2 == 1 and i == 1 and part is elo), skip_group_check=True)
                mm.then_inc(pv_done, 1)

            def turn_tensor(pe, b, k):
                pe.wait_ge(o_ready, HEADS * b + HPG * k + HPG)
                if k == 0:
                    wait(pe, wc_used, TB * b)
                for t in range(TB):
                    mm = pe.transpose(ps[:, MISC, P * t:P * t + P], otok[:, t, P * k:P * k + P], ident[:])
                mm.then_inc(o_tr, 1)

            def wc_tensor(pe, b, t, ks=range(GROUPS)):
                if ks[0] == 0:
                    pe.wait_ge(oT_ready, GROUPS * b + GROUPS)
                for k in ks:
                    mm = pe.matmul(ps[:, MISC, :], oT[:, t, k, :], wcT[:, k, :], start=(k == 0),
                                   stop=(k == GROUPS - 1))
                if ks[-1] == GROUPS - 1:
                    mm.then_inc(wc_done, 1)

            @block.tensor
            def _(pe):
                pe.wait_ge(zero_set, 2)
                pe.wait_ge(par_in, 32)
                prepare_tensor(pe, 0, 0)
                pe.wait_ge(qlo_ready, 1)
                prepare_tensor(pe, 1, 1)
                raw_tensor(pe, 0, 0, range(16))
                pe.wait_ge(qlo_ready, 2)
                maxima_tensor(pe, 0, 0)
                raw_tensor(pe, 1, 1, range(2))
                scores_tensor(pe, 0, 0, 0)
                raw_tensor(pe, 1, 1, range(2, 8))
                pe.wait_ge(v_ready, B)

                def job_read(pe, kind, b, number):
                    if kind == "turn":
                        pe.wait_ge(oT_ready, GROUPS * b + number + 1)
                    else:
                        pe.wait_ge(wc_used, TB * b + number + 1)

                def unit(u, grp, has_prepare, has_maxima, wc_batch):
                    b = 0 if wc_batch is None else wc_batch + 1
                    for j in range(8):
                        if j < 7:
                            scores_tensor(pe, u, grp, j + 1)
                        raw_tensor(pe, *ahead(u, grp, j, has_prepare, has_maxima))
                        if j > 0:
                            pv_tensor(pe, u, grp, j - 1, b)
                        elif grp > 0:
                            pv_tensor(pe, u - 1, grp - 1, 7, b)
                        elif wc_batch is not None:
                            pv_tensor(pe, u - 1, GROUPS - 1, 7, b - 1)
                        if j == 7 and has_maxima:
                            scores_tensor(pe, u + 1, (grp + 1) % GROUPS, 0)
                        if j == 0 and has_prepare:
                            if last_job(grp, b):
                                job_read(pe, *last_job(grp, b))
                            else:
                                pe.wait_ge(mlo_ready, u + 1)
                            prepare_tensor(pe, u + 2, (grp + 2) % GROUPS)
                        if j == 2 and job(grp, 2, b):
                            if has_prepare:
                                pe.wait_ge(qlo_ready, u + 3)
                            else:
                                job_read(pe, *last_job(grp, b))
                        if j == 4 and has_maxima:
                            if job(grp, 2, b):
                                job_read(pe, *job(grp, 2, b))
                            else:
                                pe.wait_ge(qlo_ready, u + 3)
                            maxima_tensor(pe, u + 1, (grp + 1) % GROUPS)
                        if j == 6 and job(grp, 6, b):
                            if has_maxima:
                                pe.wait_ge(mlo_ready, u + 2)
                            else:
                                job_read(pe, *job(grp, 2, b))
                        started = job(grp, j - j % 2, b)
                        if started:
                            kind, jb, number = started
                            if kind == "turn" and j % 2 == 0:
                                turn_tensor(pe, jb, number)
                            if kind == "tile":
                                wc_tensor(pe, jb, number, range(2 * (j % 2), 2 * (j % 2) + 2))

                batches(pe, unit)
                pv_tensor(pe, UNITS - 1, GROUPS - 1, 7, B - 1)
                pe.wait_ge(oT_ready, GROUPS * B - 1)
                turn_tensor(pe, B - 1, GROUPS - 1)
                for t in range(TB):
                    pe.wait_ge(wc_used, TB * (B - 1) + t)
                    wc_tensor(pe, B - 1, t)

            def prepare_vector(dve, u, grp):
                dve.wait_ge(qhi_ready, u + 1)
                dve.scalar_tensor_tensor(out=qlo[:, grp % 2, :], in0=ps[:, MISC, :], scalar=ATT_SCALE,
                                         in1=flt(qhi[:, grp % 2, :]), op0=ALU.mult,
                                         op1=ALU.subtract).then_inc(qlo_ready, 1)

            def maxima_vector(dve, u, grp, steps):
                for n in steps:
                    q, t = n // TB, n % TB
                    dve.wait_ge(raw_ready, 16 * u + n + 1)
                    if n == 0:
                        wait(dve, max_tr, u - 1)
                    dve.tensor_reduce(nmax[:, grp % 2, n:n + 1], ps[:, A_BANK + n % 2, :], AX.X, ALU.max,
                                      negate=True).then_inc(max_done, 1)

            def parts_vector(dve, u, grp):
                dve.wait_ge(mhi_ready, u + 1)
                dve.tensor_tensor(mlo[:, grp % 2, :], ps[0:HPG * TB, MISC, 0:P], flt(mhi[:, grp % 2, :]),
                                  ALU.subtract).then_inc(mlo_ready, 1)

            def sum_vector(dve, u, grp, q):
                h = HPG * u + q
                dve.wait_ge(pv_done, 2 * h + 2)
                wait(dve, o_ready, h)
                out = ps[:, PV_BANK, :].rearrange("p (t n) -> p t n", t=TB)
                dve.reciprocal(rden[:], out[:, :, 3 * HD]).then_inc(rden_ready, 1)
                dve.tensor_reduce(osum[:], out[:, :, 0:3 * HD].rearrange("p t (c d) -> p t d c", c=3), AX.X,
                                  ALU.add).then_inc(sum_ready, 1)

            def head_vector(dve, u, grp, q):
                h = HPG * u + q
                dve.wait_ge(rden_ready, h + 1)
                dve.wait_ge(sum_ready, h + 1)
                at = P * grp + HD * q
                dve.tensor_tensor(otok[:, :, at:at + HD], osum[:], rden[:].unsqueeze(2).to_broadcast([P, TB, HD]),
                                  ALU.mult).then_inc(o_ready, 1)

            def wc_vector(dve, b, t):
                n = TB * b + t
                dve.wait_ge(wc_done, n + 1)
                wait(dve, x_new, n)
                dve.tensor_tensor(t_out[:], ps[:, MISC, :], bc[:], ALU.add).then_inc(wc_used, 1)
                dve.wait_ge(wc_used, n + 1)
                dve.scalar_tensor_tensor(out=x[:, bass.ds(n, 1), :], in0=t_out[:], scalar=gates[:, 1:2],
                                         in1=x[:, bass.ds(n, 1), :], op0=ALU.mult, op1=ALU.add).then_inc(x_new, 1)

            @block.vector
            def _(dve):
                with dve.Fori(0, B) as b:
                    g["row_stats"](dve, 2, b)
                dve.wait_ge(par_in, 32)
                prepare_vector(dve, 0, 0)
                prepare_vector(dve, 1, 1)
                maxima_vector(dve, 0, 0, range(16))
                parts_vector(dve, 0, 0)
                maxima_vector(dve, 1, 1, range(8))

                def split(u, j):
                    e, h, l = (m.rearrange("p i s -> p (i s)")[:, 0:CUT] for m in
                               (e32[:, j % 2, :, :], ehi[:, j % 4, :, :], elo[:, j % 4, :, :]))
                    dve.wait_ge(exp_done, 8 * u + j + 1)
                    dve.tensor_tensor(l, e, h, ALU.subtract).then_inc(lo_dve, 1)

                def unit(u, grp, has_prepare, has_maxima, wc_batch):
                    b = 0 if wc_batch is None else wc_batch + 1
                    for j in range(8):
                        if j > 0:
                            split(u, j - 1)
                        elif grp > 0 or wc_batch is not None:
                            split(u - 1, 7)
                        made = {0: last_job(grp, b), 4: job(grp, 2, b)}.get(j)
                        if made and made[0] == "tile":
                            wc_vector(dve, *made[1:])
                        if j == 6 and has_maxima:
                            parts_vector(dve, u + 1, (grp + 1) % GROUPS)
                        if j == 2 and has_prepare:
                            prepare_vector(dve, u + 2, (grp + 2) % GROUPS)
                        maxima_vector(dve, *ahead(u, grp, j, has_prepare, has_maxima))
                        head = None
                        if j % 2 == 0 and j > 0:
                            head = u, grp, j // 2 - 1
                        elif j == 0 and (grp > 0 or wc_batch is not None):
                            head = u - 1, (grp - 1) % GROUPS, HPG - 1
                        if head:
                            sum_vector(dve, *head)
                        if head:
                            head_vector(dve, *head)

                batches(dve, unit)
                split(UNITS - 1, 7)
                sum_vector(dve, UNITS - 1, GROUPS - 1, HPG - 1)
                head_vector(dve, UNITS - 1, GROUPS - 1, HPG - 1)
                for t in range(TB):
                    wc_vector(dve, B - 1, t)


def mixture(nc, a, sb, g, layer):
    x, ident, gates, xn, ps = (g[k] for k in ("x", "ident", "gates", "xn", "ps"))
    cfg = MOE[layer]
    E, K, NG, SLOTS, BIASED = cfg["E"], cfg["K"], cfg["gates"], cfg["slots"], cfg["biased"]
    PAIRS = cfg["pairs"]
    tag = f"f{layer}_"
    tanh_g = gates[:, 2 + layer:3 + layer]
    w_d = a[tag + "w"]
    W13, W2 = 2 * KD * P, D
    EC = STRIPS * SLOTS

    with ExitStack() as ctx:
        xhi = sb(ctx, tag + "xhi", [P, KD, NT * P], F32R)
        xlo = sb(ctx, tag + "xlo", [P, KD, NT * P], F32R)
        comb = sb(ctx, tag + "comb", [P, SLOTS, NT * P])
        wraw = sb(ctx, tag + "wraw", [P, 2, W13 + W2])
        if BIASED:
            b13 = sb(ctx, tag + "b13", [P, 2, 2 * PAIRS])

        def sem(name):
            return ctx.enter_context(nc.semaphore(tag + name))

        last_comb = xn[:].rearrange("p t d -> p (t d)")
        raw_in = [sem("raw_in0"), sem("raw_in1")]
        bias_in = sem("bias_in")

        with ExitStack() as pre:
            gw = sb(pre, tag + "gw", [P, KD, P])
            gwhi = sb(pre, tag + "gwhi", [P, KD, P], F32R)
            gwlo = sb(pre, tag + "gwlo", [P, KD, P], F32R)
            lgT = sb(pre, tag + "lgT", [P, S])
            lg = sb(pre, tag + "lg", [P, NT, NG])
            pr = sb(pre, tag + "pr", [P, NT, E])
            bi = sb(pre, tag + "bi", [P, NT, E])
            cw = sb(pre, tag + "cw", [P, NT, EC])
            red = sb(pre, tag + "red", [P, NT])
            rank = sb(pre, tag + "rank", [P, NT, E])
            gt = sb(pre, tag + "gt", [P, TB, E, E], BF16)
            eq = sb(pre, tag + "eq", [P, TB, E, E], BF16)
            tri = sb(pre, tag + "tri", [P, E, E])
            cwx = sb(pre, tag + "cwx", [P, 2, EC, 32])
            if BIASED:
                gb = sb(pre, tag + "gb", [P, E])
                cwx1 = sb(pre, tag + "cwx1", [P, 2, P])

            psem = {}

            def s(name):
                if name not in psem:
                    psem[name] = pre.enter_context(nc.semaphore(tag + "p_" + name))
                return psem[name]

            par_in, gw_zero = s("par"), s("gw_zero")
            xn_ready, xn_read, hi_ready, lo_ready = s("xn"), s("xn_read"), s("hi"), s("lo")
            gwhi_ready, gwlo_ready = s("gwhi"), s("gwlo")
            lgT_mm, lgT_ready, lg_tr, lg_ready = s("lgT_mm"), s("lgT"), s("lg_tr"), s("lg")
            chain, shifted, exp_done, cw_ready = s("chain"), s("shifted"), s("exp"), s("cw")
            cwx_ready, cwx_tr, comb_ready = s("cwx"), s("cwx_tr"), s("comb")
            ones_set, last_tr, last_ready = s("ones"), s("last_tr"), s("last")
            PARAMS = 16 * (3 if BIASED else 2)

            with nc.Block() as block:
                @block.sync
                def _(sp):
                    sp.dma_start(gw[:], a[tag + "gateT"].rearrange("(k p) e -> p k e", p=P)).then_inc(par_in, 16)
                    sp.dma_start(tri[:], a[f"tri{E}"].rearrange("(o a) b -> o a b", o=1)
                                 .to_broadcast([P, E, E])).then_inc(par_in, 16)
                    if BIASED:
                        sp.dma_start(gb[:], a[tag + "gb"].to_broadcast([P, E])).then_inc(par_in, 16)
                        sp.dma_start(b13[:], a[tag + "b13"]).then_inc(bias_in, 16)
                    for h in range(2):
                        sp.dma_start(wraw[:, h, :], w_d[h, :, :]).then_inc(raw_in[h], 16)

                @block.scalar
                def _(act):
                    act.wait_ge(par_in, PARAMS)
                    act.copy(gwhi[:], gw[:]).then_inc(gwhi_ready, 1)
                    g["deviation"](act, 2 * layer + 1, 0)
                    for b in range(B):
                        act.wait_ge(g["s_ln"], B * (2 * layer + 1) + b + 1)
                        for t in range(TB):
                            act.wait_ge(xn_read, TB * b + t + 1)
                            g["normalise"](act, t, TB * b + t, 2 * layer + 1, xn_ready)
                        if b + 1 < B:
                            g["deviation"](act, 2 * layer + 1, b + 1)
                        act.wait_ge(xn_read, TB * b + 2 * TB)
                        for k in range(KD):
                            act.copy(xhi[:, k, S * b:S * b + S], ps[:, 4 * (b % 2) + k, :]).then_inc(hi_ready, 1)
                    with act.Fori(0, B) as b:
                        act.wait_ge(lgT_mm, b + 1)
                        act.copy(lgT[:], ps[:, 0, :]).then_inc(lgT_ready, 1)
                    act.wait_ge(shifted, 1)
                    act.activation(pr[:], lg[:, :, 0:E], ACT.Exp).then_inc(exp_done, 1)
                    if layer == 0:
                        act.activation(red[:], lg[:, :, E], ACT.Exp, scale=-1.0).then_inc(exp_done, 1)
                    with act.Fori(0, NT // 2) as i:
                        for u in range(2):
                            T = 2 * i + u
                            act.wait_ge(cwx_tr, T + 1)
                            act.copy(comb[:, :, bass.ds(P * T, P)],
                                     ps[:, u, 0:SLOTS * P].rearrange("p (s n) -> p s n", s=SLOTS)
                                     ).then_inc(comb_ready, 1)
                            if BIASED:
                                act.wait_ge(last_tr, T + 1)
                                act.copy(last_comb[:, bass.ds(P * T, P)], ps[:, 2 + u, 0:P]).then_inc(last_ready, 1)

                @block.tensor
                def _(pe):
                    pe.sem_inc(xn_read, TB)
                    with pe.Fori(0, B // 2) as i:
                        for u in range(2):
                            b = 2 * i + u
                            pe.wait_ge(lo_ready, KD * b + KD)
                            for t in range(TB):
                                pe.wait_ge(xn_ready, TB * b + t + 1)
                                for k in range(KD):
                                    mm = pe.transpose(ps[:, 4 * u + k, P * t:P * t + P],
                                                      xn[:, t, P * k:P * k + P], ident[:])
                                mm.then_inc(xn_read, 1)
                    pe.wait_ge(gwlo_ready, 1)
                    pe.wait_ge(lo_ready, KD * B + 2 * KD)
                    with pe.Fori(0, B) as b:
                        pe.wait_ge(lg_ready, b + 1)
                        n = 0
                        for k in range(KD):
                            for w, v in ((gwhi, xhi), (gwhi, xlo), (gwlo, xhi)):
                                mm = pe.matmul(ps[:, 0, :], w[:, k, :], v[:, k, bass.ds(S * b, S)],
                                               start=(n == 0), stop=(n == 3 * KD - 1))
                                n += 1
                        mm.then_inc(lgT_mm, 1)
                        pe.wait_ge(lgT_ready, b + 1)
                        for t in range(TB):
                            mm = pe.transpose(ps[:, 1, P * t:P * t + P], lgT[:, P * t:P * t + P], ident[:])
                        mm.then_inc(lg_tr, 1)
                    with pe.Fori(0, NT // 2) as i:
                        for u in range(2):
                            T = 2 * i + u
                            pe.wait_ge(cwx_ready, T + 1)
                            pe.wait_ge(comb_ready, T + 1)
                            for q in range(SLOTS):
                                mm = pe.transpose(ps[:, u, P * q:P * q + P],
                                                  cwx[:, u, STRIPS * q:STRIPS * q + STRIPS, :]
                                                  .rearrange("p e r -> p (e r)"), ident[:])
                            mm.then_inc(cwx_tr, 1)
                            if BIASED:
                                pe.wait_ge(last_ready, T + 1)
                                pe.transpose(ps[:, 2 + u, 0:P], cwx1[:, u, :], ident[:]).then_inc(last_tr, 1)

                @block.gpsimd
                def _(pool):
                    pool.sem_inc(comb_ready, 2)
                    if BIASED:
                        pool.sem_inc(last_ready, 2)
                        pool.memset(cwx1[:, :, 0:BIAS_ROW + E + 1], 1.0)
                        pool.memset(cwx1[:, :, BIAS_ROW + E + 1:P], 0.0).then_inc(ones_set, 1)

                @block.vector
                def _(dve):
                    dve.sem_inc(lo_ready, 2 * KD)
                    dve.sem_inc(lg_ready, 1)
                    count = [0]

                    def link(ins):
                        count[0] += 1
                        ins.then_inc(chain, 1)
                        dve.wait_ge(chain, count[0])

                    g["row_stats"](dve, 2 * layer + 1, 0)
                    dve.wait_ge(gwhi_ready, 1)
                    dve.tensor_tensor(gwlo[:], gw[:], flt(gwhi[:]), ALU.subtract).then_inc(gwlo_ready, 1)
                    for b in range(B):
                        if b + 1 < B:
                            g["row_stats"](dve, 2 * layer + 1, b + 1)
                        for k in range(KD):
                            dve.wait_ge(hi_ready, KD * b + k + 1)
                            dve.tensor_tensor(xlo[:, k, S * b:S * b + S], ps[:, 4 * (b % 2) + k, :],
                                              flt(xhi[:, k, S * b:S * b + S]), ALU.subtract).then_inc(lo_ready, 1)
                    with dve.Fori(0, B) as b:
                        dve.wait_ge(lg_tr, b + 1)
                        dve.tensor_copy(lg[:, bass.ds(TB * b, TB), :],
                                        ps[:, 1, :].rearrange("p (t e) -> p t e", t=TB)[:, :, 0:NG]
                                        ).then_inc(lg_ready, 1)
                    dve.wait_ge(lg_ready, B + 1)
                    wide = [P, NT, E]
                    link(dve.tensor_reduce(red[:], lg[:, :, 0:E], AX.X, ALU.max))
                    dve.tensor_tensor(lg[:, :, 0:E], lg[:, :, 0:E], red[:].unsqueeze(2).to_broadcast(wide),
                                      ALU.subtract).then_inc(shifted, 1)
                    dve.wait_ge(exp_done, 2 if layer == 0 else 1)
                    if layer == 0:
                        link(dve.tensor_scalar(red[:], red[:], 1.0, None, ALU.add))
                        link(dve.reciprocal(red[:], red[:]))
                        link(dve.tensor_copy(cw[:, :, E:E + 4], red[:].unsqueeze(2).to_broadcast([P, NT, 4])))
                    link(dve.tensor_reduce(red[:], pr[:], AX.X, ALU.add))
                    link(dve.reciprocal(red[:], red[:]))
                    link(dve.tensor_tensor(pr[:], pr[:], red[:].unsqueeze(2).to_broadcast(wide), ALU.mult))
                    sel = pr
                    if BIASED:
                        link(dve.tensor_tensor(bi[:], pr[:], gb[:].unsqueeze(1).to_broadcast(wide), ALU.add))
                        sel = bi
                    quad = [P, TB, E, E]
                    for b in range(B):
                        v = sel[:, TB * b:TB * b + TB, :]
                        other = v.unsqueeze(2).to_broadcast(quad)
                        own = v.unsqueeze(3).to_broadcast(quad)
                        dve.tensor_tensor(gt[:], other, own, ALU.is_gt)
                        link(dve.tensor_tensor(eq[:], other, own, ALU.is_equal))
                        link(dve.tensor_tensor(eq[:], eq[:], tri[:].unsqueeze(1).to_broadcast(quad), ALU.mult))
                        link(dve.tensor_tensor(gt[:], gt[:], eq[:], ALU.add))
                        link(dve.tensor_reduce(rank[:, TB * b:TB * b + TB, :], gt[:], AX.X, ALU.add))
                    link(dve.scalar_tensor_tensor(out=cw[:, :, 0:E], in0=rank[:], scalar=float(K), in1=pr[:],
                                                  op0=ALU.is_lt, op1=ALU.mult))
                    if layer == 0:
                        link(dve.tensor_reduce(red[:], cw[:, :, 0:E], AX.X, ALU.add))
                        link(dve.reciprocal(red[:], red[:]))
                        link(dve.tensor_tensor(cw[:, :, 0:E], cw[:, :, 0:E],
                                               red[:].unsqueeze(2).to_broadcast(wide), ALU.mult))
                    if BIASED:
                        dve.wait_ge(ones_set, 1)
                    with dve.Fori(0, NT // 2) as i:
                        for u in range(2):
                            T = 2 * i + u
                            dve.wait_ge(comb_ready, T + 1)
                            if BIASED:
                                dve.wait_ge(last_ready, T + 1)
                                dve.tensor_copy(cwx1[:, u, BIAS_ROW:BIAS_ROW + E], cw[:, T, 0:E])
                            dve.tensor_copy(cwx[:, u, :, :], cw[:, T, 0:EC].unsqueeze(2).to_broadcast([P, EC, 32])
                                            ).then_inc(cwx_ready, 1)

        experts(nc, a, sb, g, layer, ctx, sem, xhi, xlo, comb, wraw, b13 if BIASED else None, raw_in, bias_in, last_comb)


def experts(nc, a, sb, g, layer, ctx, sem, xhi, xlo, comb, wraw, b13, raw_in, bias_in, last_comb):
    x, gates, ps = (g[k] for k in ("x", "gates", "ps"))
    cfg = MOE[layer]
    BIASED, PAIRS = cfg["biased"], cfg["pairs"]
    tag = f"f{layer}_"
    tanh_g = gates[:, 2 + layer:3 + layer]
    w_d = a[tag + "w"]
    W13 = 2 * KD * P

    w13hi = sb(ctx, tag + "w13hi", [P, 2, 2, KD, P], F32R)
    w13lo = sb(ctx, tag + "w13lo", [P, 2, 2, KD, P], F32R)
    w2hi = sb(ctx, tag + "w2hi", [P, 2, D], F32R)
    w2lo = sb(ctx, tag + "w2lo", [P, 2, D], F32R)
    hid = sb(ctx, tag + "hid", [P, 2, S])
    ahi = sb(ctx, tag + "ahi", [P, 2, 2, S], F32R)
    alo = sb(ctx, tag + "alo", [P, 2, 2, S], F32R)

    if BIASED:
        bias13 = sb(ctx, tag + "bias13", [P, 2, 2])
        bias_ready = sem("bias")

    w13hi_ready, w13_ready, w2hi_ready, w2_ready = sem("w13hi"), sem("w13"), sem("w2hi"), sem("w2")
    raw_free = [sem("raw_free0"), sem("raw_free1")]
    gate_mm, up_mm, silu_done, comb_done, act_done = (
        sem(n) for n in ("gate_mm", "up_mm", "silu", "combined", "act"))
    ahi_ready, alo_ready, down_mm, down_used = sem("ahi"), sem("alo"), sem("down_mm"), sem("down_used")
    out_done = sem("out_done")
    ORDER = "U0 U1 D0 U2 D1 U3 D2 D3".split()

    def loops():
        p0, c0 = 0, 0
        for n, slots in cfg["loops"]:
            yield p0, n, slots, c0
            p0 += n
            c0 += 0 if slots is None else n * 2 * B

    with nc.Block() as block:
        @block.sync
        def _(sp):
            with sp.Fori(1, PAIRS) as p:
                for h in range(2):
                    sp.wait_ge(raw_free[h], p)
                    sp.dma_start(wraw[:, h, :], w_d[bass.ds(2 * p + h, 1), :, :].rearrange("o p n -> p (o n)")).then_inc(raw_in[h], 16)
            if layer == 1:
                for t in range(NT // TB):
                    sp.wait_ge(down_used, 4 + NT * (PAIRS - 1) + TB * t + TB)
                    sp.dma_start(g["out_d"][:, TB * t:TB * t + TB, :],
                                 x[:, TB * t:TB * t + TB, :]).then_inc(out_done, 16)
                sp.wait_ge(out_done, 16 * (NT // TB))

        @block.scalar
        def _(act):
            def up(p, t):
                n = B * p + t
                for h in range(2):
                    if BIASED and t == 0 and h == 0:
                        act.wait_ge(bias_ready, p + 1)
                    act.wait_ge(gate_mm, 2 * n + h + 1)
                    act.wait_ge(alo_ready, 2 * n + h + 1)
                    bias = bias13[:, 0, h:h + 1] if BIASED else 0.0
                    act.activation(hid[:, h, :], ps[:, 2 * h, :], ACT.Silu, bias=bias).then_inc(silu_done, 1)
                for h in range(2):
                    act.wait_ge(act_done, 2 * n + 2 + h + 1)
                    act.wait_ge(down_mm, 4 * n + 4)
                    act.copy(ahi[:, t % 2, h, :], hid[:, h, :]).then_inc(ahi_ready, 1)

            for p0, n_pairs, slots, c0 in loops():
                with act.Fori(0, n_pairs) as i:
                    p = i + p0
                    for h in range(2):
                        act.wait_ge(raw_in[h], 16 * p + 16)
                        act.wait_ge(up_mm, 2 * B * p + h + 1)
                        act.copy(w13hi[:, h, :, :, :].rearrange("p w k m -> p (w k m)"),
                                 wraw[:, h, 0:W13]).then_inc(w13hi_ready, 1)
                    up(p, 0)
                    act.wait_ge(down_mm, 4 * B * p + 8)
                    for h in range(2):
                        act.copy(w2hi[:, h, :], wraw[:, h, W13:W13 + D]).then_inc(w2hi_ready, 1)
                    for t in range(1, B):
                        up(p, t)

        @block.gpsimd
        def _(pool):
            for p0, n_pairs, slots, c0 in loops():
                with pool.Fori(0, n_pairs) as i:
                    p = i + p0
                    for h in range(2):
                        pool.wait_ge(w13hi_ready, 2 * p + h + 1)
                        pool.tensor_tensor(w13lo[:, h, :, :, :].rearrange("p w k m -> p (w k m)"),
                                           wraw[:, h, 0:W13],
                                           flt(w13hi[:, h, :, :, :].rearrange("p w k m -> p (w k m)")),
                                           ALU.subtract).then_inc(w13_ready, 1)
                    for t in range(B):
                        if slots is not None:
                            for h in range(2):
                                pool.wait_ge(silu_done, 2 * B * p + 2 * t + h + 1)
                                if slots[h] is None:
                                    pool.sem_inc(comb_done, 1)
                                    continue
                                tile = last_comb if slots[h] == "last" else comb[:, slots[h], :]
                                pool.tensor_tensor(hid[:, h, :], hid[:, h, :], tile[:, S * t:S * t + S],
                                                   ALU.mult).then_inc(comb_done, 1)
                        if t == 0:
                            for h in range(2):
                                pool.wait_ge(w2hi_ready, 2 * p + h + 1)
                                pool.tensor_tensor(w2lo[:, h, :], wraw[:, h, W13:W13 + D], flt(w2hi[:, h, :]),
                                                   ALU.subtract).then_inc(w2_ready, 1)
                                pool.wait_ge(w2_ready, 2 * p + h + 1)
                                pool.sem_inc(raw_free[h], 1)

        @block.vector
        def _(dve):
            dve.sem_inc(alo_ready, 2)
            dve.sem_inc(act_done, 2)
            dve.sem_inc(down_used, 4)
            if BIASED:
                dve.wait_ge(bias_in, 16)

            def up(p, t, slots, c0, p0):
                n = B * p + t
                for h in range(2):
                    dve.wait_ge(up_mm, 2 + 2 * n + h + 1)
                    if slots is None:
                        dve.wait_ge(silu_done, 2 * n + h + 1)
                    else:
                        dve.wait_ge(comb_done, c0 + 2 * B * (p - p0) + 2 * t + h + 1)
                    if BIASED:
                        dve.scalar_tensor_tensor(out=hid[:, h, :], in0=ps[:, 2 * h + 1, :],
                                                 scalar=bias13[:, 1, h:h + 1], in1=hid[:, h, :],
                                                 op0=ALU.add, op1=ALU.mult).then_inc(act_done, 1)
                    else:
                        dve.tensor_tensor(hid[:, h, :], ps[:, 2 * h + 1, :], hid[:, h, :],
                                          ALU.mult).then_inc(act_done, 1)
                for h in range(2):
                    dve.wait_ge(act_done, 2 * n + 2 + h + 1)
                    dve.wait_ge(ahi_ready, 2 * n + h + 1)
                    dve.tensor_tensor(alo[:, t % 2, h, :], hid[:, h, :], flt(ahi[:, t % 2, h, :]),
                                      ALU.subtract).then_inc(alo_ready, 1)

            def down(p, t):
                n = B * p + t
                for c in range(TB):
                    dve.wait_ge(down_mm, 8 + 4 * n + c + 1)
                    dve.wait_ge(down_used, 4 * n + c + 1)
                    dve.scalar_tensor_tensor(out=x[:, TB * t + c, :], in0=ps[:, 4 + c, :], scalar=tanh_g,
                                             in1=x[:, TB * t + c, :], op0=ALU.mult,
                                             op1=ALU.add).then_inc(down_used, 1)

            for p0, n_pairs, slots, c0 in loops():
                with dve.Fori(0, n_pairs) as i:
                    if BIASED:
                        dve.wait_ge(act_done, 2 * B * (i + p0) + 2)
                        dve.tensor_scalar(bias13[:], b13[:, :, bass.ds(2 * (i + p0), 2)], 1.0, None,
                                          ALU.mult).then_inc(bias_ready, 1)
                        dve.wait_ge(bias_ready, i + p0 + 1)
                    for what in ORDER:
                        if what[0] == "U":
                            up(i + p0, int(what[1]), slots, c0, p0)
                        else:
                            down(i + p0, int(what[1]))

        @block.tensor
        def _(pe):
            pe.sem_inc(up_mm, 2)
            pe.sem_inc(down_mm, 8)

            def up(p, t):
                n = B * p + t
                for h in range(2):
                    if t == 0:
                        pe.wait_ge(w13_ready, 2 * p + h + 1)
                    pe.wait_ge(act_done, 2 * n + h + 1)
                    for w in range(2):
                        m = 0
                        for k in range(KD):
                            for wt, xt in ((w13hi, xhi), (w13hi, xlo), (w13lo, xhi)):
                                mm = pe.matmul(ps[:, 2 * h + w, :], wt[:, h, w, k, :], xt[:, k, S * t:S * t + S],
                                               start=(m == 0), stop=(m == 3 * KD - 1))
                                m += 1
                        mm.then_inc(up_mm if w else gate_mm, 1)

            def down(p, t):
                n = B * p + t
                if t == 0:
                    pe.wait_ge(w2_ready, 2 * p + 2)
                pe.wait_ge(alo_ready, 2 * n + 4)
                for c in range(TB):
                    pe.wait_ge(down_used, 4 * n + c + 1)
                    m = 0
                    for h in range(2):
                        for at, wt in ((ahi, w2hi), (ahi, w2lo), (alo, w2hi)):
                            mm = pe.matmul(ps[:, 4 + c, :], at[:, t % 2, h, P * c:P * c + P], wt[:, h, :],
                                           start=(m == 0), stop=(m == 5))
                            m += 1
                    mm.then_inc(down_mm, 1)

            for p0, n_pairs, slots, c0 in loops():
                with pe.Fori(0, n_pairs) as i:
                    for what in ORDER:
                        (up if what[0] == "U" else down)(i + p0, int(what[1]))


def strip_chunks(w, e0, n_blocks):
    cols = w.shape[2]
    part = w[e0:e0 + 8].reshape(2, STRIPS, n_blocks, 32, cols)
    return part.transpose(2, 0, 1, 3, 4).reshape(2 * n_blocks, P, cols)


def plain_chunks(w, chunks, last_rows=None):
    full = np.zeros((chunks * P, w.shape[1]), w.dtype)
    full[:w.shape[0]] = w
    if last_rows is not None:
        at = (chunks - 1) * P + BIAS_ROW
        full[at:at + last_rows.shape[0]] = last_rows
    return full.reshape(chunks, P, w.shape[1])


def pack(w1, w3, w2, s1, s3, s2, n_blocks, shared_chunks, b2=None):
    def rows(w, sh, last_rows=None):
        parts = [strip_chunks(w, e0, n_blocks) for e0 in range(0, w.shape[0], 8)]
        return np.concatenate(parts + [plain_chunks(sh, shared_chunks, last_rows)])

    def flip(r):
        c = r.shape[0]
        return r.transpose(0, 2, 1).reshape(c, KD, P, P).transpose(0, 2, 1, 3).reshape(c, P, KD * P)

    return np.concatenate([flip(rows(w1, s1)), flip(rows(w3, s3)), rows(w2.transpose(0, 2, 1), s2.T, b2)], axis=2)


def kernel(**inputs):
    import numpy as _np
    import concourse.bacc as _bacc
    from concourse import mybir as _mybir
    from concourse.bass_utils import run_bass_kernel_spmd as _run

    v = {k: _np.asarray(w) for k, w in inputs.items()}
    arrays = {
        "x": v["x"], "ctx_512": v["ctx_512"], "ctxT": v["ctx_512"].transpose(0, 2, 1),
        "g_xattn": v["g_xattn"].reshape(1, 2), "g_ffn": v["g_ffn"].reshape(1, 2),
        "a0_wT": v["L0_xattn_W_k"].T, "a0_b": v["L0_xattn_b_k"].reshape(P, 1),
        "a0_gamma": v["L0_xattn_ln_gamma"].reshape(1, S), "a0_beta": v["L0_xattn_ln_beta"].reshape(1, S),
        "a1_wcT": v["L1_xattn_Wc"].T, "a1_bc": v["L1_xattn_bc"].reshape(1, D),
        "ident": _np.eye(P, dtype=_np.float32),
        "tri8": _np.tril(_np.ones((8, 8), _np.float32), -1),
        "tri16": _np.tril(_np.ones((16, 16), _np.float32), -1),
    }
    f0, f1 = MOE
    gu = v["L0_ffn_gate_up_proj"]
    H0 = f0["H"]
    arrays["f0_w"] = pack(gu[:, :H0], gu[:, H0:], v["L0_ffn_down_proj"], v["L0_ffn_shared_gate_w"],
                          v["L0_ffn_shared_up_w"], v["L0_ffn_shared_down_w"], H0 // 32, f0["HS"] // P)
    shared_chunks = -(-f1["HS"] // P)
    arrays["f1_w"] = pack(v["L1_ffn_w1"], v["L1_ffn_w3"], v["L1_ffn_w2"], v["L1_ffn_ws1"],
                          v["L1_ffn_ws3"], v["L1_ffn_ws2"], f1["H"] // 32, shared_chunks,
                          _np.concatenate([v["L1_ffn_b2"], v["L1_ffn_bs2"][None]]))

    def bias(e, s, one):
        parts = [strip_chunks(e[:, :, None], e0, f1["H"] // 32) for e0 in range(0, e.shape[0], 8)]
        return _np.concatenate(parts + [plain_chunks(s[:, None], shared_chunks,
                                                     _np.full((f1["E"] + 1, 1), one, s.dtype))])[:, :, 0].T

    arrays["f1_b13"] = _np.stack([bias(v["L1_ffn_b1"], v["L1_ffn_bs1"], 64.0),
                                  bias(v["L1_ffn_b3"], v["L1_ffn_bs3"], 1.0 / 64)], axis=1)
    arrays["f1_gb"] = v["L1_ffn_gate_b"].reshape(1, 16)

    def gate_columns(*ws):
        full = _np.zeros((D, P), _np.float32)
        w = _np.concatenate(ws).T
        full[:, :w.shape[1]] = w
        return full

    arrays["f0_gateT"] = gate_columns(v["L0_ffn_gate_w"], v["L0_ffn_shared_expert_gate_w"])
    arrays["f1_gateT"] = gate_columns(v["L1_ffn_gate_w"])

    nc = _bacc.Bacc("TRN2", target_bir_lowering=False, num_devices=1)
    feeds, args = {}, {}
    for name, arr in arrays.items():
        arr = _np.ascontiguousarray(arr)
        feeds[f"in_{name}_dram"] = arr
        args[name] = nc.dram_tensor(f"in_{name}_dram", arr.shape, _mybir.dt.from_np(arr.dtype),
                                    kind="ExternalInput").ap()
    args["out"] = nc.dram_tensor("out_0_dram", (B, S, D), _mybir.dt.float32, kind="ExternalOutput").ap()
    build(nc, args)
    r = _run(nc, [feeds], core_ids=[0])
    return r.results[0]["out_0_dram"]
```

```python
from contextlib import ExitStack

import numpy as np
import concourse.bass as bass
from concourse import mybir

F32 = mybir.dt.float32
F32R = mybir.dt.float32r
BF16 = mybir.dt.bfloat16
F16 = mybir.dt.float16
ALU = mybir.AluOpType
ACT = mybir.ActivationFunctionType
AX = mybir.AxisListType

P = 128
B, S, D = 4, 512, 512
NT = B * S // P
TB = S // P
KD = D // P
DC = 128
HEADS, GROUPS, HD = 16, 4, 32
HPG = HEADS // GROUPS
LN_EPS = 1e-5
SIM_EPS = 1e-6
SIM_SCALE = float(S) ** -0.5
ATT_SCALE = float(HD) ** -0.5
BIAS_ROW = 64
STRIPS = 4

MOE = [
    dict(E=8, K=2, H=192, HS=1024, gates=9, slots=3, biased=False,
         loops=[(6, (0, 1)), (4, (2, 2))]),
    dict(E=16, K=6, H=352, HS=704, gates=16, slots=4, biased=True,
         loops=[(11, (0, 1)), (11, (2, 3)), (2, None), (1, (None, "last"))]),
]
for m in MOE:
    m["pairs"] = sum(n for n, _ in m["loops"])


def flt(ap):
    return ap.bitcast(F32)


def build(nc, a):
    x_d = a["x"].rearrange("b (t p) d -> p (b t) d", p=P)
    out_d = a["out"].rearrange("b (t p) d -> p (b t) d", p=P)

    with ExitStack() as ctx:
        def sb(stack, name, shape, dt=F32):
            return stack.enter_context(nc.sbuf_tensor(name, shape, dt))

        x = sb(ctx, "x_res", [P, NT, D])
        ident = sb(ctx, "ident", [P, P])
        gates = sb(ctx, "gates", [P, 4])
        stats = sb(ctx, "stats", [P, NT, 6])
        eps = sb(ctx, "eps", [P, 2])
        msum = sb(ctx, "msum", [P, TB])
        mdif = sb(ctx, "mdif", [P, TB])
        vraw = sb(ctx, "vraw", [P, TB])
        std = sb(ctx, "std", [P, TB])
        inv = sb(ctx, "inv", [P, TB])
        rstd = sb(ctx, "rstd", [P, NT])
        nbias = sb(ctx, "nbias", [P, NT])
        xn = sb(ctx, "xn", [P, TB, D])
        ps = ctx.enter_context(nc.psum_tensor("ps", [P, 8, 512], F32))

        s_stats, s_small, s_var, s_std, s_ln = (
            ctx.enter_context(nc.semaphore(n)) for n in ("ln_stats", "ln_small", "ln_var", "ln_std", "ln_ready"))

        def row_stats(dve, nth, b):
            n = B * nth + b
            at = bass.ds(TB * b, TB)
            for t in range(TB):
                dve.bn_stats(stats[:, bass.ds(TB * b + t, 1), :], x[:, bass.ds(TB * b + t, 1), :]).then_inc(s_stats, 1)
            dve.wait_ge(s_stats, TB * n + TB)
            dve.tensor_tensor(msum[:], stats[:, at, 1], stats[:, at, 4], ALU.add)
            dve.tensor_tensor(mdif[:], stats[:, at, 1], stats[:, at, 4], ALU.subtract)
            dve.tensor_tensor(vraw[:], stats[:, at, 2], stats[:, at, 5], ALU.add).then_inc(s_small, 1)
            dve.wait_ge(s_small, 3 * n + 1)
            dve.tensor_tensor(mdif[:], mdif[:], mdif[:], ALU.mult).then_inc(s_small, 1)
            dve.wait_ge(s_small, 3 * n + 2)
            dve.scalar_tensor_tensor(out=vraw[:], in0=mdif[:], scalar=D / 4.0, in1=vraw[:],
                                     op0=ALU.mult, op1=ALU.add).then_inc(s_var, 1)
            dve.wait_ge(s_std, n + 1)
            dve.reciprocal(inv[:], std[:]).then_inc(s_small, 1)
            dve.wait_ge(s_small, 3 * n + 3)
            dve.tensor_scalar(rstd[:, at], inv[:], 1.0, None, ALU.mult)
            dve.scalar_tensor_tensor(out=nbias[:, at], in0=msum[:], scalar=-0.5, in1=inv[:],
                                     op0=ALU.mult, op1=ALU.mult).then_inc(s_ln, 1)
            dve.wait_ge(s_ln, n + 1)

        def deviation(act, nth, b):
            act.wait_ge(s_var, B * nth + b + 1)
            act.activation(std[:], vraw[:], ACT.Sqrt, scale=1.0 / D, bias=eps[:, 0:1]).then_inc(s_std, 1)

        def normalise(act, t, T, nth, s_xn):
            act.wait_ge(s_ln, B * nth + 1)
            act.activation(xn[:, t, :], x[:, T, :], ACT.Identity, scale=rstd[:, bass.ds(T, 1)],
                           bias=nbias[:, bass.ds(T, 1)]).then_inc(s_xn, 1)

        cross_attention_0(nc, a, sb, locals())
        for layer in range(2):
            if layer == 1:
                cross_attention_1(nc, a, sb, locals())
            mixture(nc, a, sb, locals(), layer)


def cross_attention_0(nc, a, sb, g):
    x, ident, gates, eps, xn, ps = (g[k] for k in ("x", "ident", "gates", "eps", "xn", "ps"))
    with ExitStack() as ctx:
        ctxT = sb(ctx, "a0_ctxT", [P, B, S])
        wkT = sb(ctx, "a0_wkT", [P, DC])
        bk = sb(ctx, "a0_bk", [P, 1])
        gamma = sb(ctx, "a0_gamma", [P, S])
        beta = sb(ctx, "a0_beta", [P, S])
        graw = sb(ctx, "a0_graw", [P, 4])
        kvT = sb(ctx, "a0_kvT", [P, S])
        kv = sb(ctx, "a0_kv", [P, TB, DC])
        pT = sb(ctx, "a0_pT", [P, KD, S])
        oT = sb(ctx, "a0_oT", [P, S])
        y = sb(ctx, "a0_y", [P, TB, S])
        st = sb(ctx, "a0_st", [P, TB, 6])
        m_sum = sb(ctx, "a0_msum", [P, TB])
        m_dif = sb(ctx, "a0_mdif", [P, TB])
        v_raw = sb(ctx, "a0_vraw", [P, TB])
        s_dev = sb(ctx, "a0_sdev", [P, TB])
        r_std = sb(ctx, "a0_rstd", [P, TB])
        n_bias = sb(ctx, "a0_nbias", [P, TB])
        mx = sb(ctx, "a0_mx", [P, TB])
        nmx = sb(ctx, "a0_nmx", [P, TB])
        den = sb(ctx, "a0_den", [P, TB])
        rden = sb(ctx, "a0_rden", [P, TB])
        coef = sb(ctx, "a0_coef", [P, TB])

        def sem(name):
            return ctx.enter_context(nc.semaphore("a0_" + name))

        x_in, par_in = [sem(f"x_in{b}") for b in range(B)], sem("par_in")
        gates_ready, gamma_done = sem("gates"), sem("gamma_done")
        xn_ready, xn_read = sem("xn"), sem("xn_read")
        kvT_mm, kvT_ready, kv_tr, kv_ready = sem("kvT_mm"), sem("kvT"), sem("kv_tr"), sem("kv")
        pT_ready, oT_mm, oT_ready = sem("pT"), sem("oT_mm"), sem("oT")
        sim_ready, sim_used = sem("sim"), sem("sim_used")
        eps_set, scale_in = sem("eps_set"), sem("scale_in")
        st_done, chain, svar, sdev_ready = sem("st"), sem("chain"), sem("svar"), sem("sdev")
        scaled, nmx_ready, exp_done, x_new = sem("scaled"), sem("nmx"), sem("exp"), sem("x_new")

        with nc.Block() as block:
            @block.sync
            def _(sp):
                def rows(b):
                    sp.dma_start(x[:, TB * b:TB * b + TB, :],
                                 g["x_d"][:, TB * b:TB * b + TB, :]).then_inc(x_in[b], 16)

                rows(0)
                sp.dma_start(ident[:], a["ident"]).then_inc(par_in, 16)
                sp.dma_start(wkT[:], a["a0_wT"]).then_inc(par_in, 16)
                sp.dma_start(bk[:], a["a0_b"]).then_inc(par_in, 16)
                sp.dma_start(ctxT[:], a["ctxT"].rearrange("b d s -> d b s")).then_inc(par_in, 16)
                for b in range(1, B):
                    rows(b)
                sp.dma_start(graw[:, 0:2], a["g_xattn"].to_broadcast([P, 2])).then_inc(scale_in, 16)
                sp.dma_start(graw[:, 2:4], a["g_ffn"].to_broadcast([P, 2])).then_inc(scale_in, 16)
                sp.dma_start(gamma[:], a["a0_gamma"].to_broadcast([P, S])).then_inc(scale_in, 16)
                sp.dma_start(beta[:], a["a0_beta"].to_broadcast([P, S])).then_inc(scale_in, 16)

            PARAMS, SCALES = 16 * 4, 16 * 4

            @block.gpsimd
            def _(pool):
                pool.memset(eps[:, 0:1], LN_EPS)
                pool.memset(eps[:, 1:2], SIM_EPS).then_inc(eps_set, 1)

            def normalise_scalar(act, b):
                act.wait_ge(g["s_ln"], b + 1)
                for t in range(TB):
                    act.wait_ge(xn_read, TB * b + t + 1)
                    g["normalise"](act, t, TB * b + t, 0, xn_ready)

            def keys_scalar(act, b):
                act.wait_ge(kvT_mm, b + 1)
                act.wait_ge(sim_ready, TB * b + TB)
                act.activation(kvT[:], ps[:, 4, :], ACT.Identity, bias=bk[:, 0:1]).then_inc(kvT_ready, 1)
                act.wait_ge(kv_tr, b + 1)
                act.copy(kv[:].rearrange("p t d -> p (t d)"), ps[:, 5, :]).then_inc(kv_ready, 1)

            def turn_scalar(act, b):
                act.wait_ge(xn_read, TB * b + 2 * TB)
                for k in range(KD):
                    act.copy(pT[:, k, :], ps[:, 4 + k, :]).then_inc(pT_ready, 1)

            def product_scalar(act, b):
                act.wait_ge(oT_mm, b + 1)
                act.mul(oT[:], ps[:, 4, :], SIM_SCALE).then_inc(oT_ready, 1)

            def deviation_scalar(act, b):
                act.wait_ge(svar, b + 1)
                act.activation(s_dev[:], v_raw[:], ACT.Sqrt, scale=1.0 / S, bias=eps[:, 1:2]).then_inc(sdev_ready, 1)

            def exp_scalar(act, b):
                for t in range(TB):
                    act.wait_ge(nmx_ready, TB * b + t + 1)
                    act.activation(y[:, t, :], y[:, t, :], ACT.Exp, bias=nmx[:, t:t + 1],
                                   accum_out=den[:, t:t + 1]).then_inc(exp_done, 1)

            @block.scalar
            def _(act):
                act.wait_ge(eps_set, 1)
                g["deviation"](act, 0, 0)
                act.wait_ge(par_in, PARAMS)
                normalise_scalar(act, 0)
                keys_scalar(act, 0)
                g["deviation"](act, 0, 1)
                g["deviation"](act, 0, 2)
                turn_scalar(act, 0)
                g["deviation"](act, 0, 3)
                act.wait_ge(scale_in, SCALES)
                act.activation(gates[:], graw[:], ACT.Tanh).then_inc(gates_ready, 1)
                product_scalar(act, 0)
                with act.Fori(0, B - 1) as b:
                    normalise_scalar(act, b + 1)
                    deviation_scalar(act, b)
                    keys_scalar(act, b + 1)
                    turn_scalar(act, b + 1)
                    exp_scalar(act, b)
                    product_scalar(act, b + 1)
                deviation_scalar(act, B - 1)
                exp_scalar(act, B - 1)

            @block.tensor
            def _(pe):
                pe.sem_inc(xn_read, TB)
                pe.sem_inc(sim_ready, TB)
                pe.wait_ge(par_in, PARAMS)
                with pe.Fori(0, B) as b:
                    pe.matmul(ps[:, 4, :], wkT[:], ctxT[:, b, :], start=True, stop=True).then_inc(kvT_mm, 1)
                    pe.wait_ge(kvT_ready, b + 1)
                    for c in range(TB):
                        mm = pe.transpose(ps[:, 5, P * c:P * c + P], kvT[:, P * c:P * c + P], ident[:])
                    mm.then_inc(kv_tr, 1)
                    pe.wait_ge(kv_ready, b + 1)
                    for t in range(TB):
                        pe.wait_ge(xn_ready, TB * b + t + 1)
                        for k in range(KD):
                            mm = pe.transpose(ps[:, 4 + k, P * t:P * t + P], xn[:, t, P * k:P * k + P], ident[:])
                        mm.then_inc(xn_read, 1)
                    pe.wait_ge(pT_ready, KD * b + KD)
                    for k in range(KD):
                        mm = pe.matmul(ps[:, 4, :], kv[:, k, :], pT[:, k, :], start=(k == 0), stop=(k == KD - 1))
                    mm.then_inc(oT_mm, 1)
                    pe.wait_ge(oT_ready, b + 1)
                    for t in range(TB):
                        pe.wait_ge(sim_used, TB * b + t + 1)
                        pe.matmul(ps[:, t, :], oT[:, P * t:P * t + P], kvT[:], start=True,
                                  stop=True).then_inc(sim_ready, 1)

            @block.vector
            def _(dve):
                dve.sem_inc(sim_used, TB)
                for b in range(B):
                    dve.wait_ge(x_in[b], 16)
                    g["row_stats"](dve, 0, b)
                dve.wait_ge(scale_in, SCALES)
                dve.wait_ge(gates_ready, 1)
                with dve.Fori(0, B) as b:
                    for t in range(TB):
                        dve.wait_ge(sim_ready, TB * b + TB + t + 1)
                        dve.bn_stats(st[:, t, :], ps[:, t, :]).then_inc(st_done, 1)
                    dve.wait_ge(st_done, TB * b + TB)
                    dve.tensor_tensor(m_sum[:], st[:, :, 1], st[:, :, 4], ALU.add)
                    dve.tensor_tensor(m_dif[:], st[:, :, 1], st[:, :, 4], ALU.subtract)
                    dve.tensor_tensor(v_raw[:], st[:, :, 2], st[:, :, 5], ALU.add).then_inc(chain, 1)
                    dve.wait_ge(chain, 8 * b + 1)
                    dve.tensor_tensor(m_dif[:], m_dif[:], m_dif[:], ALU.mult).then_inc(chain, 1)
                    dve.wait_ge(chain, 8 * b + 2)
                    dve.scalar_tensor_tensor(out=v_raw[:], in0=m_dif[:], scalar=S / 4.0, in1=v_raw[:],
                                             op0=ALU.mult, op1=ALU.add).then_inc(svar, 1)
                    dve.wait_ge(sdev_ready, b + 1)
                    dve.reciprocal(r_std[:], s_dev[:]).then_inc(chain, 1)
                    dve.wait_ge(chain, 8 * b + 3)
                    dve.scalar_tensor_tensor(out=n_bias[:], in0=m_sum[:], scalar=-0.5, in1=r_std[:],
                                             op0=ALU.mult, op1=ALU.mult).then_inc(chain, 1)
                    dve.wait_ge(chain, 8 * b + 4)
                    for h in range(2):
                        tiles = range(2 * h, 2 * h + 2)
                        for t in tiles:
                            dve.tensor_scalar(y[:, t, :], ps[:, t, :], r_std[:, t:t + 1], n_bias[:, t:t + 1],
                                              ALU.mult, ALU.add).then_inc(sim_used, 1)
                        for t in tiles:
                            dve.wait_ge(sim_used, TB * b + TB + t + 1)
                            dve.tensor_tensor(y[:, t, :], y[:, t, :], gamma[:], ALU.mult).then_inc(scaled, 1)
                        dve.wait_ge(scaled, 8 * b + 4 * h + 2)
                        dve.sem_inc(gamma_done, 1)
                        for t in tiles:
                            dve.tensor_tensor_reduce(y[:, t, :], y[:, t, :], beta[:], 1.0, -3.0e38, ALU.add,
                                                     ALU.max, mx[:, t:t + 1]).then_inc(scaled, 1)
                        for n, t in enumerate(tiles):
                            dve.wait_ge(scaled, 8 * b + 4 * h + 2 + n + 1)
                            dve.tensor_scalar(nmx[:, t:t + 1], mx[:, t:t + 1], -1.0, None,
                                              ALU.mult).then_inc(nmx_ready, 1)
                    for h in range(2):
                        pair = slice(2 * h, 2 * h + 2)
                        dve.wait_ge(exp_done, TB * b + 2 * h + 2)
                        dve.reciprocal(rden[:, pair], den[:, pair]).then_inc(chain, 1)
                        dve.wait_ge(chain, 8 * b + 2 * h + 5)
                        dve.tensor_scalar(coef[:, pair], rden[:, pair], gates[:, 0:1], None,
                                          ALU.mult).then_inc(chain, 1)
                        dve.wait_ge(chain, 8 * b + 2 * h + 6)
                        for t in range(2 * h, 2 * h + 2):
                            dve.scalar_tensor_tensor(out=x[:, TB * b + t, :], in0=y[:, t, :],
                                                     scalar=coef[:, t:t + 1], in1=x[:, TB * b + t, :],
                                                     op0=ALU.mult, op1=ALU.add).then_inc(x_new, 1)
                    dve.wait_ge(x_new, TB * b + TB)


def cross_attention_1(nc, a, sb, g):
    x, ident, gates, rstd, nbias, ps = (g[k] for k in ("x", "ident", "gates", "rstd", "nbias", "ps"))
    UNITS = B * GROUPS
    VC = 3 * HD + 1
    A_BANK, PV_BANK, MISC = 4, 6, 7
    CUT = 256
    with ExitStack() as ctx:
        qs = sb(ctx, "a1_qs", [P, HEADS, S], F32R)
        ks = sb(ctx, "a1_ks", [P, GROUPS, S], F32R)
        kraw = sb(ctx, "a1_kraw", [3 * HD, 2, S])
        xc = sb(ctx, "a1_xc", [P, 2, TB, P])
        qhi = sb(ctx, "a1_qhi", [P, 2, S], F32R)
        qlo = sb(ctx, "a1_qlo", [P, 2, S], F32R)
        vraw = sb(ctx, "a1_vraw", [P, NT, DC])
        vres = sb(ctx, "a1_vres", [P, NT, DC])
        v3 = sb(ctx, "a1_v3", [P, NT, GROUPS, VC + 1], BF16)
        nmax = sb(ctx, "a1_nmax", [P, 2, HPG * TB])
        mhi = sb(ctx, "a1_mhi", [HPG * TB, 2, P], F32R)
        mlo = sb(ctx, "a1_mlo", [HPG * TB, 2, P], F32R)
        e32 = sb(ctx, "a1_e32", [P, 4, 2, S])
        ehi = sb(ctx, "a1_ehi", [P, 4, 2, S], F16)
        elo = sb(ctx, "a1_elo", [P, 4, 2, S], F16)
        osum = sb(ctx, "a1_osum", [P, TB, HD])
        rden = sb(ctx, "a1_rden", [P, TB])
        otok = sb(ctx, "a1_otok", [P, TB, D])
        oT = sb(ctx, "a1_oT", [P, TB, GROUPS, P])
        wcT = sb(ctx, "a1_wcT", [P, KD, D])
        bc = sb(ctx, "a1_bc", [P, D])
        t_out = sb(ctx, "a1_tout", [P, D])

        def sem(name):
            return ctx.enter_context(nc.semaphore("a1_" + name))

        par_in, zero_set = sem("par_in"), sem("zero")
        v_in = sem("v_in")
        k_in, strips_in, m_in = ([sem(f"{n}{i}") for i in range(2)] for n in ("k_in", "strips_in", "m_in"))
        xc_free, scaled, xc_ready, q_tr, qhi_ready, qlo_ready = (
            sem(n) for n in ("xc_free", "scaled", "xc", "q_tr", "qhi", "qlo"))
        khi_ready, klo_ready, vhi_ready, vres_ready, vmid_ready, v_ready = (
            sem(n) for n in ("khi", "klo", "vhi", "vres", "vmid", "v"))
        raw_ready, max_done, max_tr, mhi_ready, mlo_ready = (
            sem(n) for n in ("raw", "max", "max_tr", "mhi", "mlo"))
        sc_ready, exp_done, lo_dve, lo_pool, pv_done = (
            sem(n) for n in ("sc", "exp", "lo_dve", "lo_pool", "pv"))
        rden_ready, sum_ready, o_ready = sem("rden"), sem("osum"), sem("o")
        o_tr, oT_ready, wc_done, wc_used, x_new = (sem(n) for n in ("o_tr", "oT", "wc", "wc_used", "x_new"))

        def wait(eng, s, value):
            if not isinstance(value, int) or value > 0:
                eng.wait_ge(s, value)

        def turn(u, grp):
            return (u - grp % 2) // 2 + 1

        def ahead(u, grp, j, has_prepare, has_maxima):
            if j < 4:
                return (u + 1, (grp + 1) % GROUPS, range(2 * j + 8, 2 * j + 10)) if has_maxima else (0, 0, ())
            return (u + 2, (grp + 2) % GROUPS, range(2 * j - 8, 2 * j - 6)) if has_prepare else (0, 0, ())

        JOBS = {(2, 6): ("turn", 0, 0), (3, 2): ("turn", 0, 1), (3, 6): ("turn", 0, 2), (0, 2): ("turn", 1, 3),
                (0, 6): ("tile", 1, 0), (1, 2): ("tile", 1, 1), (1, 6): ("tile", 1, 2), (2, 2): ("tile", 1, 3)}

        def job(grp, j, b):
            kind, back, number = JOBS.get((grp, j), (None, 0, 0))
            return None if kind is None or (isinstance(b, int) and b < back) else (kind, b - back, number)

        def last_job(grp, b):
            return job(grp - 1, 6, b) if grp > 0 else None if isinstance(b, int) and b < 1 else job(3, 6, b - 1)

        def batches(eng, unit):
            for grp in range(GROUPS):
                unit(grp, grp, True, True, None)
            with eng.Fori(1, B - 1) as b:
                for grp in range(GROUPS):
                    unit(GROUPS * b + grp, grp, True, True, b - 1)
            for grp in range(GROUPS):
                u = GROUPS * (B - 1) + grp
                unit(u, grp, u + 2 < UNITS, u + 1 < UNITS, B - 2)

        with nc.Block() as block:
            @block.sync
            def _(sp):
                kT_d = a["ctxT"].rearrange("b (g d) s -> (b g) d s", g=GROUPS)

                def load(u, grp):
                    wait(sp, klo_ready, u - 1)
                    for i in range(3):
                        sp.dma_start(kraw[HD * i:HD * i + HD, grp % 2, :],
                                     kT_d[bass.ds(u, 1), :, :].rearrange("o d s -> d (o s)")
                                     ).then_inc(k_in[grp % 2], 16)

                def strips(u, grp):
                    sp.wait_ge(qhi_ready, u + 1)
                    heads = slice(HPG * grp, HPG * grp + HPG)
                    for i in range(2):
                        sp.dma_start(flt(qs[HD * i:HD * i + HD, heads, :]),
                                     flt(qhi[:, grp % 2, :])).then_inc(strips_in[grp % 2], 16)
                    sp.wait_ge(qlo_ready, u + 1)
                    sp.dma_start(flt(qs[2 * HD:3 * HD, heads, :]),
                                 flt(qlo[:, grp % 2, :])).then_inc(strips_in[grp % 2], 16)

                def maxima(u, grp):
                    sp.wait_ge(mlo_ready, u + 1)
                    for i, m in enumerate((mhi, mlo)):
                        sp.dma_start(flt(qs[3 * HD + i:3 * HD + i + 1, HPG * grp:HPG * grp + HPG, :]),
                                     flt(m[:, grp % 2, :])).then_inc(m_in[grp % 2], 16)

                load(0, 0)
                load(1, 1)
                for b in range(B):
                    sp.dma_start(vraw[:, TB * b:TB * b + TB, :],
                                 a["ctx_512"][b, :, :].rearrange("(t p) d -> p t d", p=P)).then_inc(v_in, 16)
                sp.dma_start(wcT[:], a["a1_wcT"].rearrange("(k p) n -> p k n", p=P)).then_inc(par_in, 16)
                sp.dma_start(bc[:], a["a1_bc"].to_broadcast([P, D])).then_inc(par_in, 16)
                strips(0, 0)
                strips(1, 1)
                maxima(0, 0)

                def unit(u, grp, has_prepare, has_maxima, wc_batch):
                    if has_prepare:
                        load(u + 2, (grp + 2) % GROUPS)
                        strips(u + 2, (grp + 2) % GROUPS)
                    if has_maxima:
                        maxima(u + 1, (grp + 1) % GROUPS)

                batches(sp, unit)

            def prepare_pool(pool, u, grp, b):
                wait(pool, q_tr, u - 1)
                pool.sem_inc(xc_free, 1)
                wide = [P, TB, P]
                pool.tensor_tensor(xc[:, grp % 2, :, :].rearrange("p t (d q) -> p t d q", q=HPG),
                                   x[:, bass.ds(TB * b, TB), P * grp:P * grp + P]
                                   .rearrange("p t (q d) -> p t d q", q=HPG),
                                   rstd[:, bass.ds(TB * b, TB)].unsqueeze(2).unsqueeze(3)
                                   .to_broadcast([P, TB, HD, HPG]),
                                   ALU.mult).then_inc(scaled, 1)
                pool.wait_ge(scaled, u + 1)
                pool.sem_inc(xc_free, 1)
                pool.tensor_tensor(xc[:, grp % 2, :, :], xc[:, grp % 2, :, :],
                                   nbias[:, bass.ds(TB * b, TB)].unsqueeze(2).to_broadcast(wide),
                                   ALU.add).then_inc(xc_ready, 1)

            def keys_pool(pool, u, grp):
                pool.wait_ge(khi_ready, u + 1)
                pool.tensor_tensor(ks[HD:2 * HD, grp, :], kraw[HD:2 * HD, grp % 2, :], flt(ks[HD:2 * HD, grp, :]),
                                   ALU.subtract).then_inc(klo_ready, 1)
                pool.wait_ge(klo_ready, u + 1)

            v_raw, v_res = (m[:].rearrange("p t (g d) -> p t g d", g=GROUPS) for m in (vraw, vres))
            v_hi, v_mid, v_lo = (v3[:, :, :, HD * i:HD * i + HD] for i in range(3))

            @block.gpsimd
            def _(pool):
                pool.memset(flt(ks[3 * HD:3 * HD + 2, :, :]), 1.0).then_inc(zero_set, 1)
                pool.wait_ge(zero_set, 1)
                pool.memset(v3[:, :, :, 3 * HD:3 * HD + 2], 1.0).then_inc(zero_set, 1)
                pool.wait_ge(zero_set, 2)
                pool.wait_ge(g["s_ln"], 2 * B + 1)
                for u in range(2):
                    prepare_pool(pool, u, u, 0)
                pool.wait_ge(xc_ready, 2)
                keys_pool(pool, 0, 0)
                keys_pool(pool, 1, 1)
                pool.wait_ge(vhi_ready, 1)
                pool.tensor_tensor(v_res, v_raw, v_hi, ALU.subtract).then_inc(vres_ready, 1)
                prepare_pool(pool, 2, 2, 0)
                pool.wait_ge(vmid_ready, 1)
                pool.tensor_tensor(v_lo, v_res, v_mid, ALU.subtract).then_inc(v_ready, 1)
                pool.wait_ge(g["s_ln"], 2 * B + B)

                def unit(u, grp, has_prepare, has_maxima, wc_batch):
                    has_columns = has_prepare and not (isinstance(u, int) and u + 3 == UNITS)
                    for j in range(8):
                        n = 8 * u + j
                        pool.wait_ge(exp_done, n + 1)
                        e, h, l = (m.rearrange("p i s -> p (i s)")[:, CUT:] for m in
                                   (e32[:, j % 4, :, :], ehi[:, j % 4, :, :], elo[:, j % 4, :, :]))
                        pool.tensor_tensor(l, e, h, ALU.subtract).then_inc(lo_pool, 1)
                        if j == 5 and has_columns:
                            b3 = (0 if wc_batch is None else wc_batch + 1) + (grp + 3) // GROUPS
                            prepare_pool(pool, u + 3, (grp + 3) % GROUPS, b3)
                        if j == 1 and has_prepare:
                            pool.wait_ge(lo_pool, n + 1)
                            keys_pool(pool, u + 2, (grp + 2) % GROUPS)

                batches(pool, unit)

            def keys_scalar(act, u, grp):
                act.wait_ge(k_in[grp % 2], 48 * turn(u, grp))
                act.copy(ks[0:3 * HD, grp, :], kraw[:, grp % 2, :]).then_inc(khi_ready, 1)

            def prepare_scalar(act, u, grp):
                act.wait_ge(q_tr, u + 1)
                wait(act, strips_in[grp % 2], 48 * (turn(u, grp) - 1))
                act.mul(qhi[:, grp % 2, :], ps[:, MISC, :], ATT_SCALE).then_inc(qhi_ready, 1)

            def maxima_scalar(act, u, grp):
                act.wait_ge(max_tr, u + 1)
                wait(act, m_in[grp % 2], 32 * (turn(u, grp) - 1))
                act.copy(mhi[:, grp % 2, :], ps[0:HPG * TB, MISC, 0:P]).then_inc(mhi_ready, 1)

            def turn_scalar(act, b, k):
                act.wait_ge(o_tr, GROUPS * b + k + 1)
                act.copy(oT[:, :, k, :], ps[:, MISC, :].rearrange("p (t s) -> p t s", t=TB)).then_inc(oT_ready, 1)

            @block.scalar
            def _(act):
                keys_scalar(act, 0, 0)
                keys_scalar(act, 1, 1)
                prepare_scalar(act, 0, 0)
                act.wait_ge(v_in, 16 * B)
                act.copy(v_hi, v_raw).then_inc(vhi_ready, 1)
                prepare_scalar(act, 1, 1)
                g["deviation"](act, 2, 2)
                act.wait_ge(vres_ready, 1)
                act.copy(v_mid, v_res).then_inc(vmid_ready, 1)
                maxima_scalar(act, 0, 0)
                g["deviation"](act, 2, 3)

                def unit(u, grp, has_prepare, has_maxima, wc_batch):
                    b = 0 if wc_batch is None else wc_batch + 1
                    for j in range(8):
                        n = 8 * u + j
                        wait(act, lo_dve, n - 3)
                        wait(act, lo_pool, n - 3)
                        act.wait_ge(sc_ready, n + 1)
                        act.activation(e32[:, j % 4, :, :], ps[:, 2 * (j % 2):2 * (j % 2) + 2, :],
                                       ACT.Exp)
                        wait(act, pv_done, n - 3)
                        act.activation(ehi[:, j % 4, :, :], ps[:, 2 * (j % 2):2 * (j % 2) + 2, :],
                                       ACT.Exp).then_inc(exp_done, 1)
                        if j in (3, 7) and job(grp, j - 1, b) and job(grp, j - 1, b)[0] == "turn":
                            turn_scalar(act, *job(grp, j - 1, b)[1:])
                        if j == 0 and has_prepare:
                            keys_scalar(act, u + 2, (grp + 2) % GROUPS)
                        if j == 1 and has_prepare:
                            prepare_scalar(act, u + 2, (grp + 2) % GROUPS)
                        if j == 5 and has_maxima:
                            maxima_scalar(act, u + 1, (grp + 1) % GROUPS)

                batches(act, unit)
                turn_scalar(act, B - 1, GROUPS - 1)
                for b in range(B - 1):
                    g["deviation"](act, 3, b)

            def prepare_tensor(pe, u, grp):
                pe.wait_ge(xc_ready, u + 1)
                for t in range(TB):
                    mm = pe.transpose(ps[:, MISC, P * t:P * t + P], xc[:, grp % 2, t, :], ident[:])
                mm.then_inc(q_tr, 1)

            def raw_tensor(pe, u, grp, steps):
                for n in steps:
                    q, t = n // TB, n % TB
                    if n == 0:
                        pe.wait_ge(strips_in[grp % 2], 48 * turn(u, grp))
                        pe.wait_ge(klo_ready, u + 1)
                    wait(pe, max_done, 16 * u + n - 1)
                    pe.matmul(ps[:, A_BANK + n % 2, :], qs[0:3 * HD, HPG * grp + q, P * t:P * t + P],
                              ks[0:3 * HD, grp, :], start=True, stop=True).then_inc(raw_ready, 1)

            def maxima_tensor(pe, u, grp):
                pe.wait_ge(max_done, 16 * u + 16)
                pe.transpose(ps[0:HPG * TB, MISC, 0:P], nmax[:, grp % 2, :], ident[:]).then_inc(max_tr, 1)

            def scores_tensor(pe, u, grp, j):
                n = 8 * u + j
                if j == 0:
                    pe.wait_ge(m_in[grp % 2], 32 * turn(u, grp))
                wait(pe, exp_done, n - 1)
                for i in range(2):
                    c = 2 * (j % 2) + i
                    mm = pe.matmul(ps[:, 2 * (j % 2) + i, :], ks[0:3 * HD + 2, grp, P * c:P * c + P],
                                   qs[0:3 * HD + 2, HPG * grp + j // 2, :], start=True, stop=True)
                mm.then_inc(sc_ready, 1)

            def pv_tensor(pe, u, grp, j, b):
                n = 8 * u + j
                if j % 2 == 0:
                    wait(pe, sum_ready, 4 * u + j // 2)
                pe.wait_ge(lo_dve, n + 1)
                pe.wait_ge(lo_pool, n + 1)
                for t in range(TB):
                    for i in range(2):
                        for part in (ehi, elo):
                            mm = pe.matmul(ps[:, PV_BANK, P * t:P * t + VC], part[:, j % 4, i, P * t:P * t + P],
                                           v3[:, bass.ds(TB * b + 2 * (j % 2) + i, 1), grp, 0:VC],
                                           start=(j % 2 == 0 and t == 0 and i == 0 and part is ehi),
                                           stop=(j % 2 == 1 and i == 1 and part is elo), skip_group_check=True)
                mm.then_inc(pv_done, 1)

            def turn_tensor(pe, b, k):
                pe.wait_ge(o_ready, HEADS * b + HPG * k + HPG)
                if k == 0:
                    wait(pe, wc_used, TB * b)
                for t in range(TB):
                    mm = pe.transpose(ps[:, MISC, P * t:P * t + P], otok[:, t, P * k:P * k + P], ident[:])
                mm.then_inc(o_tr, 1)

            def wc_tensor(pe, b, t, ks=range(GROUPS), bank=MISC):
                if ks[0] == 0:
                    pe.wait_ge(oT_ready, GROUPS * b + GROUPS)
                for k in ks:
                    mm = pe.matmul(ps[:, bank, :], oT[:, t, k, :], wcT[:, k, :], start=(k == 0),
                                   stop=(k == GROUPS - 1))
                if ks[-1] == GROUPS - 1:
                    mm.then_inc(wc_done, 1)

            @block.tensor
            def _(pe):
                pe.wait_ge(zero_set, 2)
                prepare_tensor(pe, 0, 0)
                pe.wait_ge(qlo_ready, 1)
                prepare_tensor(pe, 1, 1)
                raw_tensor(pe, 0, 0, range(16))
                pe.wait_ge(qlo_ready, 2)
                maxima_tensor(pe, 0, 0)
                raw_tensor(pe, 1, 1, range(2))
                scores_tensor(pe, 0, 0, 0)
                raw_tensor(pe, 1, 1, range(2, 8))
                pe.wait_ge(v_ready, 1)
                pe.wait_ge(par_in, 32)

                def job_read(pe, kind, b, number):
                    if kind == "turn":
                        pe.wait_ge(oT_ready, GROUPS * b + number + 1)
                    else:
                        pe.wait_ge(wc_used, TB * b + number + 1)

                def unit(u, grp, has_prepare, has_maxima, wc_batch):
                    b = 0 if wc_batch is None else wc_batch + 1
                    for j in range(8):
                        if j < 7:
                            scores_tensor(pe, u, grp, j + 1)
                        raw_tensor(pe, *ahead(u, grp, j, has_prepare, has_maxima))
                        if j >= 2:
                            pv_tensor(pe, u, grp, j - 2, b)
                        elif grp > 0:
                            pv_tensor(pe, u - 1, grp - 1, j + 6, b)
                        elif wc_batch is not None:
                            pv_tensor(pe, u - 1, GROUPS - 1, j + 6, b - 1)
                        if j == 7 and has_maxima:
                            scores_tensor(pe, u + 1, (grp + 1) % GROUPS, 0)
                        if j == 0 and has_prepare:
                            if last_job(grp, b):
                                job_read(pe, *last_job(grp, b))
                            else:
                                pe.wait_ge(mlo_ready, u + 1)
                            prepare_tensor(pe, u + 2, (grp + 2) % GROUPS)
                        if j == 2 and job(grp, 2, b):
                            if has_prepare:
                                pe.wait_ge(qlo_ready, u + 3)
                            else:
                                job_read(pe, *last_job(grp, b))
                        if j == 4 and has_maxima:
                            if job(grp, 2, b):
                                job_read(pe, *job(grp, 2, b))
                            else:
                                pe.wait_ge(qlo_ready, u + 3)
                            maxima_tensor(pe, u + 1, (grp + 1) % GROUPS)
                        if j == 6 and job(grp, 6, b):
                            if has_maxima:
                                pe.wait_ge(mlo_ready, u + 2)
                            else:
                                job_read(pe, *job(grp, 2, b))
                        started = job(grp, j - j % 2, b)
                        if started:
                            kind, jb, number = started
                            if kind == "turn" and j % 2 == 0:
                                turn_tensor(pe, jb, number)
                            if kind == "tile":
                                wc_tensor(pe, jb, number, range(2 * (j % 2), 2 * (j % 2) + 2))

                batches(pe, unit)
                pv_tensor(pe, UNITS - 1, GROUPS - 1, 6, B - 1)
                pv_tensor(pe, UNITS - 1, GROUPS - 1, 7, B - 1)
                pe.wait_ge(oT_ready, GROUPS * B - 1)
                turn_tensor(pe, B - 1, GROUPS - 1)
                for t in range(TB):
                    wc_tensor(pe, B - 1, t, bank=t)

            def prepare_vector(dve, u, grp):
                dve.wait_ge(qhi_ready, u + 1)
                dve.scalar_tensor_tensor(out=qlo[:, grp % 2, :], in0=ps[:, MISC, :], scalar=ATT_SCALE,
                                         in1=flt(qhi[:, grp % 2, :]), op0=ALU.mult,
                                         op1=ALU.subtract).then_inc(qlo_ready, 1)

            def maxima_vector(dve, u, grp, steps):
                for n in steps:
                    q, t = n // TB, n % TB
                    dve.wait_ge(raw_ready, 16 * u + n + 1)
                    if n == 0:
                        wait(dve, max_tr, u - 1)
                    dve.tensor_reduce(nmax[:, grp % 2, n:n + 1], ps[:, A_BANK + n % 2, :], AX.X, ALU.max,
                                      negate=True).then_inc(max_done, 1)

            def parts_vector(dve, u, grp):
                dve.wait_ge(mhi_ready, u + 1)
                dve.tensor_tensor(mlo[:, grp % 2, :], ps[0:HPG * TB, MISC, 0:P], flt(mhi[:, grp % 2, :]),
                                  ALU.subtract).then_inc(mlo_ready, 1)

            def sum_vector(dve, u, grp, q):
                h = HPG * u + q
                dve.wait_ge(pv_done, 2 * h + 2)
                wait(dve, o_ready, h)
                out = ps[:, PV_BANK, :].rearrange("p (t n) -> p t n", t=TB)
                dve.reciprocal(rden[:], out[:, :, 3 * HD]).then_inc(rden_ready, 1)
                dve.tensor_reduce(osum[:], out[:, :, 0:3 * HD].rearrange("p t (c d) -> p t d c", c=3), AX.X,
                                  ALU.add).then_inc(sum_ready, 1)

            def head_vector(dve, u, grp, q):
                h = HPG * u + q
                dve.wait_ge(rden_ready, h + 1)
                dve.wait_ge(sum_ready, h + 1)
                at = P * grp + HD * q
                dve.tensor_tensor(otok[:, :, at:at + HD], osum[:], rden[:].unsqueeze(2).to_broadcast([P, TB, HD]),
                                  ALU.mult).then_inc(o_ready, 1)

            def wc_vector(dve, b, t, bank=MISC):
                n = TB * b + t
                dve.wait_ge(wc_done, n + 1)
                wait(dve, x_new, n)
                dve.tensor_tensor(t_out[:], ps[:, bank, :], bc[:], ALU.add).then_inc(wc_used, 1)
                dve.wait_ge(wc_used, n + 1)
                dve.scalar_tensor_tensor(out=x[:, bass.ds(n, 1), :], in0=t_out[:], scalar=gates[:, 1:2],
                                         in1=x[:, bass.ds(n, 1), :], op0=ALU.mult, op1=ALU.add).then_inc(x_new, 1)

            @block.vector
            def _(dve):
                prepare_vector(dve, 0, 0)
                prepare_vector(dve, 1, 1)
                g["row_stats"](dve, 2, 2)
                maxima_vector(dve, 0, 0, range(16))
                parts_vector(dve, 0, 0)
                g["row_stats"](dve, 2, 3)
                maxima_vector(dve, 1, 1, range(8))
                dve.wait_ge(par_in, 32)

                def split(u, j):
                    e, h, l = (m.rearrange("p i s -> p (i s)")[:, 0:CUT] for m in
                               (e32[:, j % 4, :, :], ehi[:, j % 4, :, :], elo[:, j % 4, :, :]))
                    dve.wait_ge(exp_done, 8 * u + j + 1)
                    dve.tensor_tensor(l, e, h, ALU.subtract).then_inc(lo_dve, 1)

                def unit(u, grp, has_prepare, has_maxima, wc_batch):
                    b = 0 if wc_batch is None else wc_batch + 1
                    for j in range(8):
                        if j > 0:
                            split(u, j - 1)
                        elif grp > 0 or wc_batch is not None:
                            split(u - 1, 7)
                        head = None
                        if j in (4, 6):
                            head = u, grp, j // 2 - 2
                        elif j in (0, 2) and (grp > 0 or wc_batch is not None):
                            head = u - 1, (grp - 1) % GROUPS, j // 2 + 2
                        if head:
                            sum_vector(dve, *head)
                        made = {0: last_job(grp, b), 4: job(grp, 2, b)}.get(j)
                        if made and made[0] == "tile":
                            wc_vector(dve, *made[1:])
                        if j == 6 and has_maxima:
                            parts_vector(dve, u + 1, (grp + 1) % GROUPS)
                        if j == 2 and has_prepare:
                            prepare_vector(dve, u + 2, (grp + 2) % GROUPS)
                        maxima_vector(dve, *ahead(u, grp, j, has_prepare, has_maxima))
                        if head:
                            head_vector(dve, *head)

                batches(dve, unit)
                split(UNITS - 1, 7)
                for q in (2, 3):
                    sum_vector(dve, UNITS - 1, GROUPS - 1, q)
                    head_vector(dve, UNITS - 1, GROUPS - 1, q)
                dve.wait_ge(x_new, TB * (B - 1))
                for b in range(B - 1):
                    g["row_stats"](dve, 3, b)
                for t in range(TB):
                    wc_vector(dve, B - 1, t, bank=t)


def mixture(nc, a, sb, g, layer):
    x, ident, gates, xn, ps = (g[k] for k in ("x", "ident", "gates", "xn", "ps"))
    cfg = MOE[layer]
    E, K, NG, SLOTS, BIASED = cfg["E"], cfg["K"], cfg["gates"], cfg["slots"], cfg["biased"]
    PAIRS = cfg["pairs"]
    NORMED = B - 1 if layer == 1 else 0
    tag = f"f{layer}_"
    tanh_g = gates[:, 2 + layer:3 + layer]
    w_d = a[tag + "w"]
    W13, W2 = 2 * KD * P, D
    EC = STRIPS * SLOTS

    with ExitStack() as ctx:
        xhi = sb(ctx, tag + "xhi", [P, KD, NT * P], F32R)
        xlo = sb(ctx, tag + "xlo", [P, KD, NT * P], F32R)
        comb = sb(ctx, tag + "comb", [P, SLOTS, NT * P])
        wraw = sb(ctx, tag + "wraw", [P, 2, W13 + W2])
        if BIASED:
            b13 = sb(ctx, tag + "b13", [P, 2, 2 * PAIRS])

        def sem(name):
            return ctx.enter_context(nc.semaphore(tag + name))

        last_comb = xn[:].rearrange("p t d -> p (t d)")
        raw_in = [sem("raw_in0"), sem("raw_in1")]
        bias_in, w13hi_ready, w13_ready = sem("bias_in"), sem("w13hi"), sem("w13")
        w13hi = sb(ctx, tag + "w13hi", [P, 2, 2, KD, P], F32R)
        w13lo = sb(ctx, tag + "w13lo", [P, 2, 2, KD, P], F32R)

        def split_hi(act, h):
            act.copy(w13hi[:, h, :, :, :].rearrange("p w k m -> p (w k m)"),
                     wraw[:, h, 0:W13]).then_inc(w13hi_ready, 1)

        def split_lo(pool, h):
            pool.tensor_tensor(w13lo[:, h, :, :, :].rearrange("p w k m -> p (w k m)"), wraw[:, h, 0:W13],
                               flt(w13hi[:, h, :, :, :].rearrange("p w k m -> p (w k m)")),
                               ALU.subtract).then_inc(w13_ready, 1)

        with ExitStack() as pre:
            gw = sb(pre, tag + "gw", [P, KD, P])
            gwhi = sb(pre, tag + "gwhi", [P, KD, P], F32R)
            gwlo = sb(pre, tag + "gwlo", [P, KD, P], F32R)
            lgT = sb(pre, tag + "lgT", [P, B, S])
            lg = sb(pre, tag + "lg", [P, NT, NG])
            pr = sb(pre, tag + "pr", [P, NT, E])
            bi = sb(pre, tag + "bi", [P, NT, E])
            cw = sb(pre, tag + "cw", [P, NT, EC])
            red = sb(pre, tag + "red", [P, NT])
            rank = sb(pre, tag + "rank", [P, NT, E])
            gt = sb(pre, tag + "gt", [P, TB, E, E], BF16)
            eq = sb(pre, tag + "eq", [P, TB, E, E], BF16)
            tri32 = sb(pre, tag + "tri32", [P, E, E])
            tri = sb(pre, tag + "tri", [P, E, E], BF16)
            cwx = sb(pre, tag + "cwx", [P, TB, EC, 32])
            if BIASED:
                gb = sb(pre, tag + "gb", [P, E])
                cwx1 = sb(pre, tag + "cwx1", [P, TB, P])

            psem = {}

            def s(name):
                if name not in psem:
                    psem[name] = pre.enter_context(nc.semaphore(tag + "p_" + name))
                return psem[name]

            par_in, gw_zero = s("par"), s("gw_zero")
            xn_ready, xn_read, hi_ready, lo_ready = s("xn"), s("xn_read"), s("hi"), s("lo")
            gwhi_ready, gwlo_ready = s("gwhi"), s("gwlo")
            lgT_mm, lgT_ready, lg_tr, lg_ready = s("lgT_mm"), s("lgT"), s("lg_tr"), s("lg")
            chain, shifted, exp_done, cw_ready = s("chain"), s("shifted"), s("exp"), s("cw")
            cwx_ready, cwx_tr, comb_ready = s("cwx"), s("cwx_tr"), s("comb")
            tri_ready = s("tri")
            ones_set, last_tr, last_ready = s("ones"), s("last_tr"), s("last")
            PARAMS = 16 * (3 if BIASED else 2)

            with nc.Block() as block:
                @block.sync
                def _(sp):
                    sp.dma_start(gw[:], a[tag + "gateT"].rearrange("(k p) e -> p k e", p=P)).then_inc(par_in, 16)
                    sp.dma_start(tri32[:], a[f"tri{E}"].rearrange("(o a) b -> o a b", o=1)
                                 .to_broadcast([P, E, E])).then_inc(par_in, 16)
                    if BIASED:
                        sp.dma_start(gb[:], a[tag + "gb"].to_broadcast([P, E])).then_inc(par_in, 16)
                        sp.dma_start(b13[:], a[tag + "b13"]).then_inc(bias_in, 16)
                    for h in range(2):
                        sp.dma_start(wraw[:, h, :], w_d[h, :, :]).then_inc(raw_in[h], 16)

                @block.scalar
                def _(act):
                    act.wait_ge(par_in, PARAMS)
                    act.copy(gwhi[:], gw[:]).then_inc(gwhi_ready, 1)
                    if NORMED == 0:
                        g["deviation"](act, 2 * layer + 1, 0)

                    def logits_scalar(b):
                        act.wait_ge(lgT_mm, b + 1)
                        act.copy(lgT[:, b, :], ps[:, 4 * (b % 2), :]).then_inc(lgT_ready, 1)

                    for b in range(B):
                        act.wait_ge(g["s_ln"], B * (2 * layer + 1) + b + 1)
                        for t in range(TB):
                            act.wait_ge(xn_read, TB * b + t + 1)
                            g["normalise"](act, t, TB * b + t, 2 * layer + 1, xn_ready)
                        if NORMED <= b + 1 < B:
                            g["deviation"](act, 2 * layer + 1, b + 1)
                        act.wait_ge(xn_read, TB * b + 2 * TB)
                        for k in range(KD):
                            act.copy(xhi[:, k, S * b:S * b + S], ps[:, 4 * (b % 2) + k, :]).then_inc(hi_ready, 1)
                        if b > 0:
                            logits_scalar(b - 1)
                    logits_scalar(B - 1)
                    for h in range(2):
                        act.wait_ge(raw_in[h], 16)
                        split_hi(act, h)
                    act.wait_ge(shifted, 1)
                    act.activation(pr[:], lg[:, :, 0:E], ACT.Exp).then_inc(exp_done, 1)
                    if layer == 0:
                        act.activation(red[:], lg[:, :, E], ACT.Exp, scale=-1.0).then_inc(exp_done, 1)
                    if BIASED:
                        act.wait_ge(ones_set, 1)
                    for b in range(B):
                        act.wait_ge(cw_ready, b + 1)
                        for t in range(TB):
                            T = TB * b + t
                            if b > 0:
                                act.wait_ge(cwx_tr, T - TB + 1)
                            if BIASED:
                                if b > 0:
                                    act.wait_ge(last_tr, T - TB + 1)
                                act.copy(cwx1[:, t, BIAS_ROW:BIAS_ROW + E], cw[:, T, 0:E])
                            act.copy(cwx[:, t, :, :], cw[:, T, 0:EC].unsqueeze(2).to_broadcast([P, EC, 32])
                                     ).then_inc(cwx_ready, 1)
                        for t in range(TB):
                            T = TB * b + t
                            act.wait_ge(cwx_tr, T + 1)
                            act.copy(comb[:, :, P * T:P * T + P],
                                     ps[:, t % 2, 0:SLOTS * P].rearrange("p (s n) -> p s n", s=SLOTS)
                                     ).then_inc(comb_ready, 1)
                            if BIASED:
                                act.wait_ge(last_tr, T + 1)
                                act.copy(last_comb[:, P * T:P * T + P],
                                         ps[:, 2 + t % 2, 0:P]).then_inc(last_ready, 1)

                @block.tensor
                def _(pe):
                    pe.sem_inc(xn_read, TB)

                    def logits(b):
                        pe.wait_ge(gwlo_ready, 1)
                        pe.wait_ge(lo_ready, KD * b + KD)
                        n = 0
                        for k in range(KD):
                            for w, v in ((gwhi, xhi), (gwhi, xlo), (gwlo, xhi)):
                                mm = pe.matmul(ps[:, 4 * (b % 2), :], w[:, k, :], v[:, k, S * b:S * b + S],
                                               start=(n == 0), stop=(n == 3 * KD - 1))
                                n += 1
                        mm.then_inc(lgT_mm, 1)

                    for b in range(B):
                        if b >= 2:
                            pe.wait_ge(lgT_ready, b - 1)
                        for t in range(TB):
                            pe.wait_ge(xn_ready, TB * b + t + 1)
                            for k in range(KD):
                                mm = pe.transpose(ps[:, 4 * (b % 2) + k, P * t:P * t + P],
                                                  xn[:, t, P * k:P * k + P], ident[:])
                            mm.then_inc(xn_read, 1)
                        if b > 0:
                            logits(b - 1)
                    logits(B - 1)
                    pe.wait_ge(lgT_ready, B)
                    for b in range(B):
                        for t in range(TB):
                            mm = pe.transpose(ps[:, 4 + b, P * t:P * t + P], lgT[:, b, P * t:P * t + P], ident[:])
                        mm.then_inc(lg_tr, 1)
                    with pe.Fori(0, B) as b:
                        for t in range(TB):
                            T = TB * b + t
                            pe.wait_ge(cwx_ready, T + 1)
                            pe.wait_ge(comb_ready, T + 1)
                            for q in range(SLOTS):
                                mm = pe.transpose(ps[:, t % 2, P * q:P * q + P],
                                                  cwx[:, t, STRIPS * q:STRIPS * q + STRIPS, :]
                                                  .rearrange("p e r -> p (e r)"), ident[:])
                            mm.then_inc(cwx_tr, 1)
                            if BIASED:
                                pe.wait_ge(last_ready, T + 1)
                                pe.transpose(ps[:, 2 + t % 2, 0:P], cwx1[:, t, :], ident[:]).then_inc(last_tr, 1)

                def compared(b):
                    v = (bi if BIASED else pr)[:, TB * b:TB * b + TB, :]
                    quad = [P, TB, E, E]
                    return v.unsqueeze(2).to_broadcast(quad), v.unsqueeze(3).to_broadcast(quad)

                @block.gpsimd
                def _(pool):
                    pool.sem_inc(comb_ready, 2)
                    pool.wait_ge(par_in, PARAMS)
                    pool.tensor_copy(tri[:], tri32[:]).then_inc(tri_ready, 1)
                    if BIASED:
                        pool.sem_inc(last_ready, 2)
                        pool.memset(cwx1[:, :, 0:BIAS_ROW + E + 1], 1.0)
                        pool.memset(cwx1[:, :, BIAS_ROW + E + 1:P], 0.0).then_inc(ones_set, 1)
                    for h in range(2):
                        pool.wait_ge(w13hi_ready, h + 1)
                        split_lo(pool, h)

                @block.vector
                def _(dve):
                    count = [0]

                    def link(ins):
                        count[0] += 1
                        ins.then_inc(chain, 1)
                        dve.wait_ge(chain, count[0])

                    if NORMED == 0:
                        g["row_stats"](dve, 2 * layer + 1, 0)
                    dve.wait_ge(gwhi_ready, 1)
                    dve.tensor_tensor(gwlo[:], gw[:], flt(gwhi[:]), ALU.subtract).then_inc(gwlo_ready, 1)
                    for b in range(B):
                        if NORMED <= b + 1 < B:
                            g["row_stats"](dve, 2 * layer + 1, b + 1)
                        for k in range(KD):
                            dve.wait_ge(hi_ready, KD * b + k + 1)
                            dve.tensor_tensor(xlo[:, k, S * b:S * b + S], ps[:, 4 * (b % 2) + k, :],
                                              flt(xhi[:, k, S * b:S * b + S]), ALU.subtract).then_inc(lo_ready, 1)
                    for b in range(B):
                        dve.wait_ge(lg_tr, b + 1)
                        dve.tensor_copy(lg[:, TB * b:TB * b + TB, :],
                                        ps[:, 4 + b, :].rearrange("p (t e) -> p t e", t=TB)[:, :, 0:NG]
                                        ).then_inc(lg_ready, 1)
                    dve.wait_ge(lg_ready, B)
                    wide = [P, NT, E]
                    link(dve.tensor_reduce(red[:], lg[:, :, 0:E], AX.X, ALU.max))
                    dve.tensor_tensor(lg[:, :, 0:E], lg[:, :, 0:E], red[:].unsqueeze(2).to_broadcast(wide),
                                      ALU.subtract).then_inc(shifted, 1)
                    dve.wait_ge(exp_done, 2 if layer == 0 else 1)
                    if layer == 0:
                        link(dve.tensor_scalar(red[:], red[:], 1.0, None, ALU.add))
                        link(dve.reciprocal(red[:], red[:]))
                        link(dve.tensor_copy(cw[:, :, E:E + 4], red[:].unsqueeze(2).to_broadcast([P, NT, 4])))
                    link(dve.tensor_reduce(red[:], pr[:], AX.X, ALU.add))
                    link(dve.reciprocal(red[:], red[:]))
                    link(dve.tensor_tensor(pr[:], pr[:], red[:].unsqueeze(2).to_broadcast(wide), ALU.mult))
                    if BIASED:
                        link(dve.tensor_tensor(bi[:], pr[:], gb[:].unsqueeze(1).to_broadcast(wide), ALU.add))
                    dve.wait_ge(tri_ready, 1)
                    quad = [P, TB, E, E]
                    for b in range(B):
                        dve.tensor_tensor(gt[:], *compared(b), ALU.is_gt)
                        link(dve.tensor_tensor(eq[:], *compared(b), ALU.is_equal))
                        link(dve.tensor_tensor(eq[:], eq[:], tri[:].unsqueeze(1).to_broadcast(quad), ALU.mult))
                        link(dve.tensor_tensor(eq[:], gt[:], eq[:], ALU.add))
                        link(dve.tensor_reduce(rank[:, TB * b:TB * b + TB, :], eq[:], AX.X, ALU.add))
                        rows = slice(TB * b, TB * b + TB)
                        link(dve.scalar_tensor_tensor(out=cw[:, rows, 0:E], in0=rank[:, rows, :], scalar=float(K),
                                                      in1=pr[:, rows, :], op0=ALU.is_lt, op1=ALU.mult))
                        if layer == 0:
                            link(dve.tensor_reduce(red[:, rows], cw[:, rows, 0:E], AX.X, ALU.add))
                            link(dve.reciprocal(red[:, rows], red[:, rows]))
                            link(dve.tensor_tensor(cw[:, rows, 0:E], cw[:, rows, 0:E], red[:, rows].unsqueeze(2)
                                                   .to_broadcast([P, TB, E]), ALU.mult))
                        dve.sem_inc(cw_ready, 1)

        experts(nc, a, sb, g, layer, ctx, sem, xhi, xlo, comb, wraw, b13 if BIASED else None, raw_in, bias_in, last_comb,
                w13hi, w13lo, w13hi_ready, w13_ready, split_hi, split_lo)


def experts(nc, a, sb, g, layer, ctx, sem, xhi, xlo, comb, wraw, b13, raw_in, bias_in, last_comb,
            w13hi, w13lo, w13hi_ready, w13_ready, split_hi, split_lo):
    x, gates, ps = (g[k] for k in ("x", "gates", "ps"))
    cfg = MOE[layer]
    BIASED, PAIRS = cfg["biased"], cfg["pairs"]
    tag = f"f{layer}_"
    tanh_g = gates[:, 2 + layer:3 + layer]
    w_d = a[tag + "w"]
    W13 = 2 * KD * P

    w2hi = sb(ctx, tag + "w2hi", [P, 2, D], F32R)
    w2lo = sb(ctx, tag + "w2lo", [P, 2, D], F32R)
    hid = sb(ctx, tag + "hid", [P, 2, S])
    ahi = sb(ctx, tag + "ahi", [P, 2, 2, S], F32R)
    alo = sb(ctx, tag + "alo", [P, 2, 2, S], F32R)

    if BIASED:
        bias13 = sb(ctx, tag + "bias13", [P, 2, 2])
        bias_ready = sem("bias")

    w2hi_ready, w2_ready = sem("w2hi"), sem("w2")
    raw_free = [sem("raw_free0"), sem("raw_free1")]
    gate_mm, up_mm, silu_done, comb_done, act_done = (
        sem(n) for n in ("gate_mm", "up_mm", "silu", "combined", "act"))
    ahi_ready, alo_ready, down_mm, down_used = sem("ahi"), sem("alo"), sem("down_mm"), sem("down_used")
    out_done = sem("out_done")
    ORDER = "U0 U1 D0 U2 D1 U3 D2 D3".split()

    def loops():
        p0, c0 = 0, 0
        for n, slots in cfg["loops"]:
            for part in ((1, n - 1) if p0 == 0 else (n,)):
                yield p0, part, slots, c0
                p0 += part
                c0 += 0 if slots is None else part * 2 * B

    def repeat(eng, p0, n_pairs, body):
        if n_pairs == 1:
            body(p0)
        elif n_pairs > 1:
            with eng.Fori(0, n_pairs) as i:
                body(i + p0)

    with nc.Block() as block:
        @block.sync
        def _(sp):
            with sp.Fori(1, PAIRS) as p:
                for h in range(2):
                    sp.wait_ge(raw_free[h], p)
                    sp.dma_start(wraw[:, h, :], w_d[bass.ds(2 * p + h, 1), :, :].rearrange("o p n -> p (o n)")).then_inc(raw_in[h], 16)
            if layer == 1:
                for t in range(NT // TB):
                    sp.wait_ge(down_used, 4 + NT * (PAIRS - 1) + TB * t + TB)
                    sp.dma_start(g["out_d"][:, TB * t:TB * t + TB, :],
                                 x[:, TB * t:TB * t + TB, :]).then_inc(out_done, 16)
                sp.wait_ge(out_done, 16 * (NT // TB))

        @block.scalar
        def _(act):
            def up(p, t):
                n = B * p + t
                for h in range(2):
                    if BIASED and t == 0 and h == 0:
                        act.wait_ge(bias_ready, p + 1)
                    act.wait_ge(gate_mm, 2 * n + h + 1)
                    act.wait_ge(alo_ready, 2 * n + h + 1)
                    bias = bias13[:, 0, h:h + 1] if BIASED else 0.0
                    act.activation(hid[:, h, :], ps[:, 2 * h, :], ACT.Silu, bias=bias).then_inc(silu_done, 1)
                for h in range(2):
                    act.wait_ge(act_done, 2 * n + 2 + h + 1)
                    act.wait_ge(down_mm, 4 * n + 4)
                    act.copy(ahi[:, t % 2, h, :], hid[:, h, :]).then_inc(ahi_ready, 1)

            def pair(p):
                if not isinstance(p, int) or p > 0:
                    for h in range(2):
                        act.wait_ge(raw_in[h], 16 * p + 16)
                        act.wait_ge(up_mm, 2 * B * p + h + 1)
                        split_hi(act, h)
                up(p, 0)
                act.wait_ge(down_mm, 4 * B * p + 8)
                for h in range(2):
                    act.copy(w2hi[:, h, :], wraw[:, h, W13:W13 + D]).then_inc(w2hi_ready, 1)
                for t in range(1, B):
                    up(p, t)

            for p0, n_pairs, slots, c0 in loops():
                repeat(act, p0, n_pairs, pair)
            if layer == 0:
                for b in range(2):
                    g["deviation"](act, 2, b)

        @block.gpsimd
        def _(pool):
            def pair(p, slots):
                if not isinstance(p, int) or p > 0:
                    for h in range(2):
                        pool.wait_ge(w13hi_ready, 2 * p + h + 1)
                        split_lo(pool, h)
                for t in range(B):
                    if slots is not None:
                        for h in range(2):
                            pool.wait_ge(silu_done, 2 * B * p + 2 * t + h + 1)
                            if slots[h] is None:
                                pool.sem_inc(comb_done, 1)
                                continue
                            tile = last_comb if slots[h] == "last" else comb[:, slots[h], :]
                            pool.tensor_tensor(hid[:, h, :], hid[:, h, :], tile[:, S * t:S * t + S],
                                               ALU.mult).then_inc(comb_done, 1)
                    if t == 0:
                        for h in range(2):
                            pool.wait_ge(w2hi_ready, 2 * p + h + 1)
                            pool.tensor_tensor(w2lo[:, h, :], wraw[:, h, W13:W13 + D], flt(w2hi[:, h, :]),
                                               ALU.subtract).then_inc(w2_ready, 1)
                            pool.wait_ge(w2_ready, 2 * p + h + 1)
                            pool.sem_inc(raw_free[h], 1)

            for p0, n_pairs, slots, c0 in loops():
                repeat(pool, p0, n_pairs, lambda p: pair(p, slots))

        @block.vector
        def _(dve):
            dve.sem_inc(alo_ready, 2)
            dve.sem_inc(act_done, 2)
            dve.sem_inc(down_used, 4)
            if BIASED:
                dve.wait_ge(bias_in, 16)

            def up(p, t, slots, c0, p0):
                n = B * p + t
                for h in range(2):
                    dve.wait_ge(up_mm, 2 + 2 * n + h + 1)
                    if slots is None:
                        dve.wait_ge(silu_done, 2 * n + h + 1)
                    else:
                        dve.wait_ge(comb_done, c0 + 2 * B * (p - p0) + 2 * t + h + 1)
                    if BIASED:
                        dve.scalar_tensor_tensor(out=hid[:, h, :], in0=ps[:, 2 * h + 1, :],
                                                 scalar=bias13[:, 1, h:h + 1], in1=hid[:, h, :],
                                                 op0=ALU.add, op1=ALU.mult).then_inc(act_done, 1)
                    else:
                        dve.tensor_tensor(hid[:, h, :], ps[:, 2 * h + 1, :], hid[:, h, :],
                                          ALU.mult).then_inc(act_done, 1)
                for h in range(2):
                    dve.wait_ge(act_done, 2 * n + 2 + h + 1)
                    dve.wait_ge(ahi_ready, 2 * n + h + 1)
                    dve.tensor_tensor(alo[:, t % 2, h, :], hid[:, h, :], flt(ahi[:, t % 2, h, :]),
                                      ALU.subtract).then_inc(alo_ready, 1)

            def down(p, t):
                n = B * p + t
                for c in range(TB):
                    dve.wait_ge(down_mm, 8 + 4 * n + c + 1)
                    dve.wait_ge(down_used, 4 * n + c + 1)
                    dve.scalar_tensor_tensor(out=x[:, TB * t + c, :], in0=ps[:, 4 + c, :], scalar=tanh_g,
                                             in1=x[:, TB * t + c, :], op0=ALU.mult,
                                             op1=ALU.add).then_inc(down_used, 1)

            def pair(p, slots, c0, p0, last):
                if BIASED:
                    dve.wait_ge(act_done, 2 * B * p + 2)
                    dve.tensor_scalar(bias13[:], b13[:, :, bass.ds(2 * p, 2)], 1.0, None,
                                      ALU.mult).then_inc(bias_ready, 1)
                    dve.wait_ge(bias_ready, p + 1)
                for what in ORDER:
                    t = int(what[1])
                    if last and what in ("D2", "D3"):
                        dve.wait_ge(down_used, 4 + NT * p + TB * (t - 1))
                        g["row_stats"](dve, 2, t - 2)
                    if what[0] == "U":
                        up(p, t, slots, c0, p0)
                    else:
                        down(p, t)

            for p0, n_pairs, slots, c0 in loops():
                rest = 1 if layer == 0 and p0 + n_pairs == PAIRS else 0
                repeat(dve, p0, n_pairs - rest, lambda p: pair(p, slots, c0, p0, False))
                if rest:
                    pair(PAIRS - 1, slots, c0, p0, True)

        @block.tensor
        def _(pe):
            pe.sem_inc(up_mm, 2)
            pe.sem_inc(down_mm, 8)

            def up(p, t):
                n = B * p + t
                for h in range(2):
                    if t == 0:
                        pe.wait_ge(w13_ready, 2 * p + h + 1)
                    pe.wait_ge(act_done, 2 * n + h + 1)
                    for w in range(2):
                        m = 0
                        for k in range(KD):
                            for wt, xt in ((w13hi, xhi), (w13hi, xlo), (w13lo, xhi)):
                                mm = pe.matmul(ps[:, 2 * h + w, :], wt[:, h, w, k, :], xt[:, k, S * t:S * t + S],
                                               start=(m == 0), stop=(m == 3 * KD - 1))
                                m += 1
                        mm.then_inc(up_mm if w else gate_mm, 1)

            def down(p, t):
                n = B * p + t
                if t == 0:
                    pe.wait_ge(w2_ready, 2 * p + 2)
                pe.wait_ge(alo_ready, 2 * n + 4)
                for c in range(TB):
                    pe.wait_ge(down_used, 4 * n + c + 1)
                    m = 0
                    for h in range(2):
                        for at, wt in ((ahi, w2hi), (ahi, w2lo), (alo, w2hi)):
                            mm = pe.matmul(ps[:, 4 + c, :], at[:, t % 2, h, P * c:P * c + P], wt[:, h, :],
                                           start=(m == 0), stop=(m == 5))
                            m += 1
                    mm.then_inc(down_mm, 1)

            def pair(p):
                for what in ORDER:
                    (up if what[0] == "U" else down)(p, int(what[1]))

            for p0, n_pairs, slots, c0 in loops():
                repeat(pe, p0, n_pairs, pair)


def strip_chunks(w, e0, n_blocks):
    cols = w.shape[2]
    part = w[e0:e0 + 8].reshape(2, STRIPS, n_blocks, 32, cols)
    return part.transpose(2, 0, 1, 3, 4).reshape(2 * n_blocks, P, cols)


def plain_chunks(w, chunks, last_rows=None):
    full = np.zeros((chunks * P, w.shape[1]), w.dtype)
    full[:w.shape[0]] = w
    if last_rows is not None:
        at = (chunks - 1) * P + BIAS_ROW
        full[at:at + last_rows.shape[0]] = last_rows
    return full.reshape(chunks, P, w.shape[1])


def pack(w1, w3, w2, s1, s3, s2, n_blocks, shared_chunks, b2=None):
    def rows(w, sh, last_rows=None):
        parts = [strip_chunks(w, e0, n_blocks) for e0 in range(0, w.shape[0], 8)]
        return np.concatenate(parts + [plain_chunks(sh, shared_chunks, last_rows)])

    def flip(r):
        c = r.shape[0]
        return r.transpose(0, 2, 1).reshape(c, KD, P, P).transpose(0, 2, 1, 3).reshape(c, P, KD * P)

    return np.concatenate([flip(rows(w1, s1)), flip(rows(w3, s3)), rows(w2.transpose(0, 2, 1), s2.T, b2)], axis=2)


def kernel(**inputs):
    import numpy as _np
    import concourse.bacc as _bacc
    from concourse import mybir as _mybir
    from concourse.bass_utils import run_bass_kernel_spmd as _run

    v = {k: _np.asarray(w) for k, w in inputs.items()}
    arrays = {
        "x": v["x"], "ctx_512": v["ctx_512"], "ctxT": v["ctx_512"].transpose(0, 2, 1),
        "g_xattn": v["g_xattn"].reshape(1, 2), "g_ffn": v["g_ffn"].reshape(1, 2),
        "a0_wT": v["L0_xattn_W_k"].T, "a0_b": v["L0_xattn_b_k"].reshape(P, 1),
        "a0_gamma": v["L0_xattn_ln_gamma"].reshape(1, S), "a0_beta": v["L0_xattn_ln_beta"].reshape(1, S),
        "a1_wcT": v["L1_xattn_Wc"].T, "a1_bc": v["L1_xattn_bc"].reshape(1, D),
        "ident": _np.eye(P, dtype=_np.float32),
        "tri8": _np.tril(_np.ones((8, 8), _np.float32), -1),
        "tri16": _np.tril(_np.ones((16, 16), _np.float32), -1),
    }
    f0, f1 = MOE
    gu = v["L0_ffn_gate_up_proj"]
    H0 = f0["H"]
    arrays["f0_w"] = pack(gu[:, :H0], gu[:, H0:], v["L0_ffn_down_proj"], v["L0_ffn_shared_gate_w"],
                          v["L0_ffn_shared_up_w"], v["L0_ffn_shared_down_w"], H0 // 32, f0["HS"] // P)
    shared_chunks = -(-f1["HS"] // P)
    arrays["f1_w"] = pack(v["L1_ffn_w1"], v["L1_ffn_w3"], v["L1_ffn_w2"], v["L1_ffn_ws1"],
                          v["L1_ffn_ws3"], v["L1_ffn_ws2"], f1["H"] // 32, shared_chunks,
                          _np.concatenate([v["L1_ffn_b2"], v["L1_ffn_bs2"][None]]))

    def bias(e, s, one):
        parts = [strip_chunks(e[:, :, None], e0, f1["H"] // 32) for e0 in range(0, e.shape[0], 8)]
        return _np.concatenate(parts + [plain_chunks(s[:, None], shared_chunks,
                                                     _np.full((f1["E"] + 1, 1), one, s.dtype))])[:, :, 0].T

    arrays["f1_b13"] = _np.stack([bias(v["L1_ffn_b1"], v["L1_ffn_bs1"], 64.0),
                                  bias(v["L1_ffn_b3"], v["L1_ffn_bs3"], 1.0 / 64)], axis=1)
    arrays["f1_gb"] = v["L1_ffn_gate_b"].reshape(1, 16)

    def gate_columns(*ws):
        full = _np.zeros((D, P), _np.float32)
        w = _np.concatenate(ws).T
        full[:, :w.shape[1]] = w
        return full

    arrays["f0_gateT"] = gate_columns(v["L0_ffn_gate_w"], v["L0_ffn_shared_expert_gate_w"])
    arrays["f1_gateT"] = gate_columns(v["L1_ffn_gate_w"])

    nc = _bacc.Bacc("TRN2", target_bir_lowering=False, num_devices=1)
    feeds, args = {}, {}
    for name, arr in arrays.items():
        arr = _np.ascontiguousarray(arr)
        feeds[f"in_{name}_dram"] = arr
        args[name] = nc.dram_tensor(f"in_{name}_dram", arr.shape, _mybir.dt.from_np(arr.dtype),
                                    kind="ExternalInput").ap()
    args["out"] = nc.dram_tensor("out_0_dram", (B, S, D), _mybir.dt.float32, kind="ExternalOutput").ap()
    build(nc, args)
    r = _run(nc, [feeds], core_ids=[0])
    return r.results[0]["out_0_dram"]
```
